# Optimizing a Trainium2 kernel written in Bass

```python
import numpy as np
import jax
import jax.numpy as jnp

def _softmax(x, axis=-1):
    return jax.nn.softmax(x, axis=axis)

def _gelu(x):
    return jax.nn.gelu(x, approximate=True)

def _silu(x):
    return jax.nn.silu(x)

def _sigmoid(x):
    return jax.nn.sigmoid(x)

def _layernorm(x, axis=-1, eps=1e-05):
    m = jnp.mean(x, axis=axis, keepdims=True)
    v = jnp.var(x, axis=axis, keepdims=True)
    return (x - m) / jnp.sqrt(v + eps)

def _scatter_add(tgt, idx, src, axis=0):
    return tgt.at[idx].add(src)

def _segment_sum(src, seg, n):
    return jax.ops.segment_sum(src, seg, n)
kernel_name = 'mk_flamingo_gated_d1_seqx_r8_39692e'

def setup_inputs(seed: int=0):
    np.random.seed(seed)
    _w = jnp.asarray

    def _rec_inputs():
        import jax
        import jax.numpy as jnp
        _rk = jax.random.key(seed)
        x = -0.0003929 + 0.9999 * jax.random.normal(jax.random.fold_in(_rk, 1), (32, 64, 512), jnp.float32)
        _lenS = 64 - jax.random.randint(jax.random.fold_in(_rk, 7), (32,), 0, max(1, 64 // 4) + 1, jnp.int32)
        _lenS2 = 64 - jax.random.randint(jax.random.fold_in(_rk, 8), (32,), 0, max(1, 64 // 4) + 1, jnp.int32)
        _ctx_1024P = jax.random.normal(jax.random.fold_in(_rk, 11), (32, 16, 128), jnp.float32)
        _ctx_1024c = jax.random.dirichlet(jax.random.fold_in(_rk, 511), 0.3 * jnp.ones((16,), jnp.float32), (32, 64))
        _ctx_1024t = jnp.einsum('bsk,bkd->bsd', _ctx_1024c, _ctx_1024P)
        _ctx_1024t = _ctx_1024t * jax.lax.rsqrt(jnp.mean(jnp.square(_ctx_1024t)) + 1e-12) * 0.953939
        ctx_1024 = -1.39393e-06 + 0.999914 * (_ctx_1024t + 0.3 * jax.random.normal(jax.random.fold_in(_rk, 611), (32, 64, 128), jnp.float32))
        _g = jax.random.normal(jax.random.fold_in(_rk, 9001), (2, 1), jnp.float32)
        _g = jnp.sign(_g) * jnp.maximum(jnp.abs(_g), 1.0) + (_g == 0) * 1.0
        g_xattn = _g[0]
        g_ffn = _g[1]
        return (x, ctx_1024, g_xattn, g_ffn)
    x, ctx_1024, g_xattn, g_ffn = _rec_inputs()

    def _L0_xattn_setup():
        import jax, jax.numpy as jnp
        import numpy as np
        import math
        DIM_V = 64
        key = jax.random.key(seed)
        k1, k2, k3, k4, k5, k6 = jax.random.split(key, 6)
        B, C, N, M = (8, DIM_V, 512, 128)
        pcd_up = jax.random.normal(k1, (B, C, N), dtype=jnp.float32)
        pcd_down = jax.random.normal(k2, (B, C, M), dtype=jnp.float32)
        s = 1.0 / math.sqrt(C)
        Wq = jax.random.normal(k3, (C, C), dtype=jnp.float32) * s
        Wk = jax.random.normal(k4, (C, C), dtype=jnp.float32) * s
        Wv = jax.random.normal(k5, (C, C), dtype=jnp.float32) * s
        Wskip = jax.random.normal(k6, (C, C), dtype=jnp.float32) * s
        return {'pcd_up': pcd_up, 'pcd_down': pcd_down, 'Wq': Wq, 'Wk': Wk, 'Wv': Wv, 'Wskip': Wskip}
    _L0_xattn_all = _L0_xattn_setup()
    _L0_xattn_in = {k: v for k, v in _L0_xattn_all.items() if k in ('Wq', 'Wk', 'Wv', 'Wskip')}
    del _L0_xattn_all

    def _L0_ffn_setup():
        import jax, jax.numpy as jnp
        import numpy as np
        B, L, H, Dh, M = (4, 256, 16, 32, 128)
        D = H * Dh
        key = jax.random.key(seed)
        kx, ku, kd, kp = jax.random.split(key, 4)
        x = jax.random.normal(kx, (B, L, D), dtype=jnp.float32)
        up = jax.random.normal(ku, (H, Dh, M), dtype=jnp.float32)
        down = jax.random.normal(kd, (H, M, Dh), dtype=jnp.float32)
        perm = jax.random.permutation(kp, D)
        return {'x': x, 'up': up, 'down': down, 'perm': perm}
    _L0_ffn_all = _L0_ffn_setup()
    _L0_ffn_in = {k: v for k, v in _L0_ffn_all.items() if k in ('up', 'down', 'perm')}
    del _L0_ffn_all
    return {'x': x, 'ctx_1024': ctx_1024, 'g_xattn': g_xattn, 'g_ffn': g_ffn, 'L0_xattn_Wq': _L0_xattn_in['Wq'], 'L0_xattn_Wk': _L0_xattn_in['Wk'], 'L0_xattn_Wv': _L0_xattn_in['Wv'], 'L0_xattn_Wskip': _L0_xattn_in['Wskip'], 'L0_ffn_up': _L0_ffn_in['up'], 'L0_ffn_down': _L0_ffn_in['down'], 'L0_ffn_perm': _L0_ffn_in['perm']}

def reference(x, ctx_1024, g_xattn, g_ffn, L0_xattn_Wq, L0_xattn_Wk, L0_xattn_Wv, L0_xattn_Wskip, L0_ffn_up, L0_ffn_down, L0_ffn_perm):
    import jax
    import jax.numpy as jnp

    def _L0_xattn_ref(pcd_up, pcd_down, Wq, Wk, Wv, Wskip):
        import jax, jax.numpy as jnp
        import numpy as np
        import math
        DIM_V = 64
        q = jnp.einsum('oc,bcn->bon', Wq, pcd_up)
        k = jnp.einsum('oc,bcm->bom', Wk, pcd_down)
        v = jnp.einsum('oc,bcm->bom', Wv, pcd_down)
        C = q.shape[1]
        scale = jnp.sqrt(jnp.asarray(C, dtype=q.dtype))
        energy = jnp.einsum('bcn,bcm->bnm', q, k) / scale
        attention = jax.nn.softmax(energy, axis=-1)
        x = jnp.einsum('bnm,bcm->bcn', attention, v)
        skip = jnp.einsum('oc,bcn->bon', Wskip, pcd_up)
        return skip + x

    def _L0_ffn_ref(x, up, down, perm):
        import jax, jax.numpy as jnp
        import numpy as np
        B, L, H, Dh, M = (4, 256, 16, 32, 128)
        D = H * Dh
        b, l, Dm = x.shape
        h, d = (up.shape[0], up.shape[1])
        unperm = jnp.argsort(perm)
        t = x.reshape(b * l, Dm)
        t = t[:, perm]
        t = t.reshape(b * l, h, d)
        t = jnp.einsum('bhd,hdm->bhm', t, up)
        t = jax.nn.gelu(t, approximate=False)
        t = jnp.einsum('bhm,hmd->bhd', t, down)
        t = t.reshape(b * l, h * d)
        t = t[:, unperm]
        out = t.reshape(b, l, Dm)
        return out
    x = x + jnp.tanh(g_xattn[0]) * _L0_xattn_ref(_layernorm(x, axis=-1), ctx_1024, L0_xattn_Wq, L0_xattn_Wk, L0_xattn_Wv, L0_xattn_Wskip)
    x = x + jnp.tanh(g_ffn[0]) * _L0_ffn_ref(_layernorm(x, axis=-1), L0_ffn_up, L0_ffn_down, L0_ffn_perm)
    return x

_drawn_inputs = setup_inputs


def setup_inputs(seed=0):
    import zlib

    import numpy as np

    out = dict(_drawn_inputs(seed))
    spreads = {}
    factors = {}
    for name, (base, spread) in spreads.items():
        noise = np.random.default_rng([zlib.crc32(name.encode()), seed]).standard_normal(out[name].shape)
        drawn = base * np.exp(spread * noise) if base else spread * noise
        out[name] = jnp.asarray(drawn.astype(out[name].dtype))
    for name, factor in factors.items():
        out[name] = (out[name] * factor).astype(out[name].dtype)
    return out
```

```python
from contextlib import ExitStack

import concourse.bass as bass
from concourse import mybir
from concourse.alu_op_type import AluOpType as ALU

ACT = mybir.ActivationFunctionType
AX = mybir.AxisListType
F32 = mybir.dt.float32
F32R = mybir.dt.float32r
I32 = mybir.dt.int32
U32 = mybir.dt.uint32

EPS = 1e-5


def build_block(nc, x_head, x_rest, ctx, perm, gates, wq, wk, wv_t, wskip_t, up, down, out):
    P = 128
    N, HEAD_ROWS = x_head.shape
    ROWS = HEAD_ROWS + x_rest.shape[1]
    M = ctx.shape[1]
    C = wq.shape[0]
    HEADS, DH, MH = up.shape
    NT = N // P
    PAIRS = ROWS // P
    CH = 512
    CHUNKS = ROWS // CH
    PPC = CH // P
    HPT = P // DH
    UNIT = 2 * 2 * M
    SCALE = 1.0 / float(C) ** 0.5

    es = ExitStack()

    def sb(name, shape, dt=F32):
        return es.enter_context(nc.sbuf_tensor(name, shape, dt))

    def sem(name):
        return es.enter_context(nc.semaphore(name))

    with es:
        xt = sb("xt", [P, NT, ROWS])
        x_rows = sb("x_rows", [P, PAIRS, N])
        stack = sb("stack", [P, 2 * NT, ROWS], F32R)
        x_stage = [sb(f"x_stage{s}", [P, NT, P]) for s in range(2)]
        ctx_stage = [sb(f"ctx_stage{s}", [P, M]) for s in range(2)]
        xn = [sb(f"xn{s}", [P, N]) for s in range(2)]
        x1 = [sb(f"x1_{s}", [P, N]) for s in range(2)]
        xn2 = [sb(f"xn2_{s}", [P, N]) for s in range(2)]
        kq = [sb(f"kq{s}", [P, 2, M]) for s in range(2)]
        vt = [sb(f"vt{s}", [P, 2, C]) for s in range(2)]
        probs = [sb(f"probs{h}", [P, 4, M]) for h in range(2)]
        pn = [[sb(f"pn{s}_{h}", [P, 4, M]) for h in range(2)] for s in range(2)]
        probs_t = [sb(f"probs_t{s}", [P, 2, NT, P]) for s in range(2)]
        high = [sb(f"high{s}", [P, NT, P], F32R) for s in range(2)]
        low = [sb(f"low{s}", [P, NT, P], F32R) for s in range(2)]
        neg_max = [sb(f"neg_max{h}", [P, 4]) for h in range(2)]
        sums = [sb(f"sums{h}", [P, 4]) for h in range(2)]
        inv_sum = [sb(f"inv_sum{h}", [P, 4]) for h in range(2)]
        bn1 = sb("bn1", [P, 6])
        bn2 = sb("bn2", [P, 6])
        stats1 = [sb(f"stats1_{s}", [P, 2]) for s in range(2)]
        stats2 = [sb(f"stats2_{s}", [P, 2]) for s in range(2)]
        var1 = sb("var1", [P, 1])
        var2 = sb("var2", [P, 1])
        rstd1 = [sb(f"rstd1_{s}", [P, 1]) for s in range(2)]
        rstd2 = [sb(f"rstd2_{s}", [P, 1]) for s in range(2)]
        minus_half = sb("minus_half", [P, 1])
        eps = sb("eps", [P, 1])
        ident = sb("ident", [P, P])
        perm_sb = sb("perm_sb", [P, NT], I32)
        out_index = sb("out_index", [P, CHUNKS, NT], I32)
        gates_sb = sb("gates_sb", [P, 2])
        tanh_g = sb("tanh_g", [P, 2])
        wq_sb = sb("wq_sb", [C, C])
        wk_sb = sb("wk_sb", [C, 2, C])
        wkq = sb("wkq", [P, 2, C])
        wv_raw = sb("wv_raw", [P, 2, C])
        wv_sb = sb("wv_sb", [P, 2 * C])
        ws_raw = sb("ws_raw", [P, 2, C])
        ws_sb = sb("ws_sb", [P, 2 * C])
        up_raw = sb("up_raw", [P, HEADS, MH])
        up_high = sb("up_high", [P, HEADS, MH], F32R)
        up_low = sb("up_low", [P, HEADS, MH], F32R)
        down_sb = sb("down_sb", [P, HEADS, DH])
        x_flat = x_rows[:, :, :].rearrange("p a n -> p (a n)")
        hidden = [x_flat[:, g * CH:(g + 1) * CH] for g in range(2 * HPT)]
        result = [x_flat[:, (2 * HPT + g) * CH:(2 * HPT + g + 1) * CH] for g in range(4)]

        bank = [es.enter_context(nc.psum_tensor(f"bank{b}", [P, 512], F32)) for b in range(8)]
        score_bank = bank[0:2]
        probs_t_bank = bank[2:4]
        x1_bank, x_bank, mix_bank, x1t_bank = bank[4:8]
        up_bank = bank[0:4]
        down_bank = [x1_bank, x_bank]

        s_perm = sem("perm_loaded")
        s_wkq = sem("wkq_loaded")
        s_gates = sem("gates_loaded")
        s_wvs = sem("wv_wskip_loaded")
        s_up = sem("up_loaded")
        s_down = sem("down_loaded")
        s_zero = sem("dve_zeroed")
        s_ident = sem("identity_made")
        s_half = sem("constants_set")
        s_index = sem("index_made")
        s_tanh = sem("tanh_made")
        s_wkq_mm = sem("wkq_multiplied")
        s_wkq_sb = sem("wkq_ready")
        s_wvs_sb = sem("wv_wskip_ready")
        s_up_high = sem("up_high_ready")
        s_up_low = sem("up_low_ready")
        s_down_sb = sem("down_ready")
        s_head = sem("x_head_gathered")
        s_rest = sem("x_rest_gathered")
        s_xstage = [sem(f"x_staged{s}") for s in range(2)]
        s_cstage = [sem(f"ctx_staged{s}") for s in range(2)]
        s_t0 = sem("x_transposed")
        s_xevac = sem("x_rows_stored")
        s_bn1a = sem("bn1_done")
        s_st1 = sem("stats1_done")
        s_var1 = sem("var1_done")
        s_rstd1 = sem("rstd1_done")
        s_xn = sem("xn_ready")
        s_kqv = sem("kq_v_multiplied")
        s_kqv_sb = sem("kq_v_stored")
        s_score = sem("scores_ready")
        s_max = sem("max_ready")
        s_exp = sem("exp_done")
        s_inv = sem("inv_sum_ready")
        s_pn = sem("probs_normalised")
        s_pt = sem("probs_transposed")
        s_pt_sb = [sem(f"probs_t_stored{h}") for h in range(2)]
        s_att = sem("attention_done")
        s_x1 = sem("x1_ready")
        s_bn2a = sem("bn2_done")
        s_st2 = sem("stats2_done")
        s_var2 = sem("var2_done")
        s_rstd2 = sem("rstd2_ready")
        s_xn2 = sem("xn2_ready")
        s_x1t = sem("x1_transposed")
        s_x1t_sb = sem("x1_t_stored")
        s_xn2t = sem("xn2_transposed")
        s_high = sem("high_ready")
        s_low = sem("low_ready")
        s_stack = [sem(f"stacked{s}") for s in range(2)]
        s_upmm = sem("up_multiplied")
        s_gelu = sem("gelu_done")
        s_downmm = sem("down_multiplied")
        s_res = sem("result_ready")
        s_out = [sem(f"result_stored{g}") for g in range(4)]

        block = es.enter_context(nc.Block())

        def pipeline(engine, step):
            for i in range(-1, 4):
                step(i, i % 2)
            with engine.Fori(2, PAIRS // 2 - 1) as k:
                for s in range(2):
                    step(2 * k + s, s)
            for i in range(PAIRS - 2, PAIRS + 2):
                step(i, i % 2)

        def has(q):
            return not isinstance(q, int) or 0 <= q < PAIRS

        def past(q, least):
            return not isinstance(q, int) or q >= least

        def pair_rows(q):
            return bass.ds(q * P, P)

        def staged(q, s):
            return 8 * (q - s) + 16

        def store_probs_t(engine, copy, q, s, h):
            if has(q):
                engine.wait_ge(s_pt, 2 * q + h + 1)
                if past(q, 2):
                    engine.wait_ge(s_att, q - 1)
                copy(probs_t[s][:, :, 2 * h:2 * h + 2, :].rearrange("m b t n -> m b (t n)"),
                     probs_t_bank[h][:, :].rearrange("m (b n) -> m b n", b=2)).then_inc(s_pt_sb[h], 1)

        @block.sync
        def _(sp):
            sp.dma_start(perm_sb[:, :], perm).then_inc(s_perm, 16)
            sp.dma_start(wq_sb[:, :], wq).then_inc(s_wkq, 16)
            sp.dma_start(gates_sb[:, :], gates.to_broadcast([P, 2])).then_inc(s_gates, 16)

            def stage(q, s):
                if has(q):
                    if past(q, 2):
                        sp.wait_ge(s_t0, q - 1)
                    sp.wait_ge(s_head if isinstance(q, int) and q < PPC else s_rest, 16 * NT)
                    sp.dma_start(x_stage[s][:, :, :], xt[:, :, pair_rows(q)]).then_inc(s_xstage[s], 16)
                    if past(q, 2):
                        sp.wait_ge(s_kqv, q - 1)
                    sp.dma_start(ctx_stage[s][:, :], ctx[pair_rows(q), :]).then_inc(s_cstage[s], 16)

            def step(i, s):
                if isinstance(i, int) and i == -1:
                    stage(0, 0)
                    for b in range(2):
                        half = slice(b * C, (b + 1) * C)
                        sp.dma_start(wv_raw[half, b, :], wv_t).then_inc(s_wvs, 16)
                        sp.dma_start(ws_raw[half, b, :], wskip_t).then_inc(s_wvs, 16)
                    stage(1, 1)
                    sp.wait_ge(s_zero, 1)
                    for b in range(2):
                        for r in range(2):
                            rows = slice(b * 2 * DH + r * DH, b * 2 * DH + (r + 1) * DH)
                            sp.dma_start(up_raw[rows, r::2, :], up[r::2, :, :].rearrange("h d m -> d h m"))\
                              .then_inc(s_up, 16)
                    sp.dma_start(down_sb[:, :, :], down.rearrange("h m d -> m h d")).then_inc(s_down, 16)
                    return
                stage(i + 2, s)
                if has(i - 2):
                    q = i - 2
                    sp.wait_ge(s_low, q + 1)
                    lo, hi = slice(0, 2 * DH), slice(2 * DH, P)
                    for dst, src, first in ((lo, (high, lo), 0), (hi, (low, lo), 0),
                                            (lo, (high, hi), 1), (hi, (low, hi), 1)):
                        part, rows = src
                        sp.dma_start(stack[dst, first::2, pair_rows(q)].bitcast(F32), part[s][rows, :, :].bitcast(F32))\
                          .then_inc(s_stack[s], 16)

            pipeline(sp, step)

        @block.gpsimd
        def _(pool):
            pool.wait_ge(s_perm, 16)
            for t in range(NT):
                pool.indirect_dma_start(
                    xt[:, t, 0:HEAD_ROWS], None, x_head,
                    bass.IndirectOffsetOnAxis(ap=perm_sb[:, t:t + 1].bitcast(U32), axis=0)).then_inc(s_head, 16)
            pool.memset(ident[:, :], 0.0).then_inc(s_ident, 1)
            pool.memset(minus_half[:, :], -0.5).then_inc(s_half, 1)
            pool.memset(eps[:, :], EPS).then_inc(s_half, 1)
            pool.wait_ge(s_ident, 1)
            pool.affine_select(out=ident[:, :], in_=ident[:, :], compare_op=ALU.not_equal, fill=1.0,
                               base=0, pattern=[[-1, P]], channel_multiplier=1).then_inc(s_ident, 1)
            for t in range(NT):
                pool.indirect_dma_start(
                    xt[:, t, HEAD_ROWS:ROWS], None, x_rest,
                    bass.IndirectOffsetOnAxis(ap=perm_sb[:, t:t + 1].bitcast(U32), axis=0)).then_inc(s_rest, 16)
            pool.wait_ge(s_half, 2)

            def rstd(var, stats, to, done_var, done, q):
                pool.tensor_tensor(var[:, :], stats[:, 1:2], eps[:, :], ALU.add).then_inc(done_var, 1)
                pool.wait_ge(done_var, q + 1)
                pool.tensor_tensor(to[:, :], var[:, :], minus_half[:, :], ALU.pow).then_inc(done, 1)

            def normalise(q, s, h):
                if has(q):
                    pool.wait_ge(s_inv, 2 * q + h + 1)
                    if past(q, 2):
                        pool.wait_ge(s_pt, 2 * q + h - 3)
                    pool.tensor_tensor(pn[s][h][:, :, :], probs[h][:, :, :],
                                       inv_sum[h][:, :].unsqueeze(2).to_broadcast([P, 4, M]),
                                       ALU.mult).then_inc(s_pn, 1)

            def step(i, s):
                normalise(i, s, 0)
                if has(i + 1):
                    q, o = i + 1, 1 - s
                    pool.wait_ge(s_st1, q + 1)
                    rstd(var1, stats1[o], rstd1[o], s_var1, s_rstd1, q)
                normalise(i, s, 1)
                if has(i - 1):
                    q, o = i - 1, 1 - s
                    pool.wait_ge(s_st2, q + 1)
                    if past(q, 2):
                        pool.wait_ge(s_xn2t, q - 1)
                    rstd(var2, stats2[o], rstd2[o], s_var2, s_rstd2, q)
                    pool.wait_ge(s_half, 2)
                    pool.wait_ge(s_rstd2, q + 1)
                    pool.tensor_scalar(xn2[o][:, :], x1[o][:, :], stats2[o][:, 0:1], rstd2[o][:, 0:1],
                                       ALU.subtract, ALU.mult).then_inc(s_xn2, 1)

            pipeline(pool, step)

            pool.wait_ge(s_index, CHUNKS)
            for c in range(CHUNKS):
                for t in range(NT):
                    tile = c * NT + t
                    pool.wait_ge(s_res, tile + 1)
                    pool.indirect_dma_start(
                        out, bass.IndirectOffsetOnAxis(ap=out_index[:, c, t:t + 1].bitcast(U32), axis=0),
                        result[tile % 4], None).then_inc(s_out[tile % 4], 16)
            for g in range(4):
                pool.wait_ge(s_out[g], 16 * CHUNKS * NT // 4)

        @block.tensor
        def _(pe):
            pe.wait_ge(s_ident, 2)
            pe.wait_ge(s_wkq, 48)
            pe.matmul(mix_bank[:, 0:C], wk_sb[:, :, :].rearrange("o b c -> o (b c)"), wq_sb[:, :],
                      start=True, stop=True).then_inc(s_wkq_mm, 1)

            def transposes(to, of, cols=P):
                for t in range(NT):
                    last = pe.transpose(to[:, t * P:(t + 1) * P], of(t), ident[:, :])
                return last

            def scores(q, s, h):
                if has(q):
                    if h == 0:
                        pe.wait_ge(s_xn, q + 1)
                        pe.wait_ge(s_kqv_sb, q + 1)
                    if past(q, 1):
                        pe.wait_ge(s_exp, 2 * q + h - 1)
                    for j in range(2):
                        t = 2 * h + j
                        last = pe.matmul(score_bank[h][:, j * 2 * M:(j + 1) * 2 * M], xn[s][:, t * P:(t + 1) * P],
                                         kq[s][:, :, :].rearrange("c b m -> c (b m)"), start=True, stop=True)
                    last.then_inc(s_score, 1)

            def probs_transposes(q, s, h):
                if has(q):
                    pe.wait_ge(s_pn, 2 * q + h + 1)
                    if past(q, 1):
                        pe.wait_ge(s_pt_sb[h], q)
                    for j in range(2):
                        for b in range(2):
                            at = (2 * b + j) * P
                            last = pe.transpose(probs_t_bank[h][:, at:at + P], pn[s][h][:, 2 * j + b, :], ident[:, :])
                    last.then_inc(s_pt, 1)

            def step(i, s):
                o = 1 - s
                scores(i, s, 0)
                probs_transposes(i - 1, o, 0)
                probs_transposes(i - 1, o, 1)
                if has(i + 1):
                    q = i + 1
                    pe.wait_ge(s_xstage[o], staged(q, o))
                    if past(q, 1):
                        pe.wait_ge(s_xevac, q)
                    transposes(x_bank, lambda t: x_stage[o][:, t, :]).then_inc(s_t0, 1)
                scores(i, s, 1)
                if has(i - 1):
                    q = i - 1
                    if past(q, 1):
                        pe.wait_ge(s_x1, q)
                    if not past(q, 1):
                        pe.wait_ge(s_wvs_sb, 2)
                    pe.matmul(x1_bank[:, :], ws_sb[:, :], xn[o][:, :], start=True, stop=False, skip_group_check=True)
                    pe.wait_ge(s_pt_sb[0], q + 1)
                    pe.wait_ge(s_pt_sb[1], q + 1)
                    for b in range(2):
                        last = pe.matmul(x1_bank[b * C:(b + 1) * C, :], vt[o][:, b, :],
                                         probs_t[o][:, b, :, :].rearrange("m t n -> m (t n)"),
                                         start=False, stop=True, skip_group_check=True)
                    last.then_inc(s_att, 1)
                if has(i + 1):
                    q = i + 1
                    pe.wait_ge(s_cstage[o], staged(q, o))
                    if past(q, 4):
                        pe.wait_ge(s_low, q - 3)
                    if not past(q, 1):
                        pe.wait_ge(s_wkq_sb, 2)
                        pe.wait_ge(s_wvs_sb, 2)
                    pe.matmul(mix_bank[:, 0:M], wkq[:, :, :].rearrange("c b e -> c (b e)"), ctx_stage[o][:, :],
                              start=True, stop=True)
                    pe.matmul(mix_bank[:, M:M + 2 * C], ctx_stage[o][:, :], wv_sb[:, :],
                              start=True, stop=True).then_inc(s_kqv, 1)
                if has(i - 2):
                    q = i - 2
                    pe.wait_ge(s_x1, q + 1)
                    if past(q, 1):
                        pe.wait_ge(s_x1t_sb, q)
                    transposes(x1t_bank, lambda t: x1[s][:, t * P:(t + 1) * P]).then_inc(s_x1t, 1)
                    pe.wait_ge(s_xn2, q + 1)
                    if has(q + 3):
                        pe.wait_ge(s_kqv_sb, q + 4)
                    else:
                        pe.wait_ge(s_low, q)
                    transposes(mix_bank, lambda t: xn2[s][:, t * P:(t + 1) * P]).then_inc(s_xn2t, 1)

            pipeline(pe, step)

            def up_tile(c, t):
                for h in range(t * HPT, (t + 1) * HPT):
                    if not isinstance(c, int) or c > 0 or h >= 4:
                        pe.wait_ge(s_gelu, c * HEADS + h - 3)
                    part = 2 * t + (h % HPT) // 2
                    for w, first in ((up_high, True), (up_low, False)):
                        last = pe.matmul(up_bank[h % 4][:, :], w[:, h, :], stack[:, part, bass.ds(c * CH, CH)],
                                         start=first, stop=not first)
                    last.then_inc(s_upmm, 1)

            def down_tile(c, t):
                pe.wait_ge(s_gelu, c * HEADS + (t + 1) * HPT)
                if not isinstance(c, int) or c > 0 or t >= 2:
                    pe.wait_ge(s_res, c * NT + t - 1)
                for g in range(HPT):
                    h = t * HPT + g
                    last = pe.matmul(down_bank[t % 2][g * DH:(g + 1) * DH, :], down_sb[:, h, :], hidden[h % (2 * HPT)],
                                     start=True, stop=True, skip_group_check=True)
                last.then_inc(s_downmm, 1)

            def chunk(c, last):
                for t in range(NT):
                    if t + 1 < NT:
                        up_tile(c, t + 1)
                    elif not last:
                        stacked(c + 1)
                        up_tile(c + 1, 0)
                    down_tile(c, t)

            def stacked(c):
                for s in range(2):
                    pe.wait_ge(s_stack[s], (c + 1) * (PPC // 2 * 4 * 16))

            pe.wait_ge(s_exp, 2 * PAIRS)
            pe.wait_ge(s_pt_sb[0], PAIRS)
            pe.wait_ge(s_pt_sb[1], PAIRS)
            pe.wait_ge(s_up_high, 1)
            pe.wait_ge(s_up_low, 1)
            stacked(0)
            up_tile(0, 0)
            pe.wait_ge(s_x1, PAIRS)
            pe.wait_ge(s_xevac, PAIRS)
            pe.wait_ge(s_down_sb, 1)
            chunk(0, False)
            with pe.Fori(1, CHUNKS - 1) as c:
                chunk(c, False)
            chunk(CHUNKS - 1, True)

        @block.scalar
        def _(act):
            for b in range(2):
                act.dma_start(wk_sb[:, b, :], wk).then_inc(s_wkq, 16)
            act.wait_ge(s_gates, 16)
            act.activation(tanh_g[:, :], gates_sb[:, :], ACT.Tanh).then_inc(s_tanh, 1)
            act.wait_ge(s_wkq_mm, 1)
            act.activation(wkq[0:C, 0, :], mix_bank[0:C, 0:C], ACT.Copy, scale=SCALE).then_inc(s_wkq_sb, 1)
            act.activation(wkq[C:P, 1, :], mix_bank[C:P, 0:C], ACT.Copy, scale=SCALE).then_inc(s_wkq_sb, 1)

            def exps(q, h):
                if has(q):
                    act.wait_ge(s_max, 2 * q + h + 1)
                    if past(q, 1):
                        act.wait_ge(s_pn, 2 * q + h - 1)
                    for g in range(4):
                        last = act.activation(probs[h][:, g, :], score_bank[h][:, g * M:(g + 1) * M], ACT.Exp,
                                              bias=neg_max[h][:, g:g + 1], accum_out=sums[h][:, g:g + 1])
                    last.then_inc(s_exp, 1)

            def step(i, s):
                o = 1 - s
                if has(i + 1):
                    act.wait_ge(s_t0, i + 2)
                    act.activation(x_rows[:, bass.ds(i + 1, 1), :],
                                   x_bank[:, :].rearrange("p (a n) -> p a n", a=1), ACT.Copy).then_inc(s_xevac, 1)
                exps(i, 0)
                store_probs_t(act, act.copy, i - 1, o, 1)
                if has(i + 1):
                    q = i + 1
                    act.wait_ge(s_kqv, q + 1)
                    if past(q, 2):
                        act.wait_ge(s_score, 2 * q - 2)
                        act.wait_ge(s_att, q - 1)
                    if not past(q, 1):
                        act.wait_ge(s_zero, 1)
                    for b in range(2):
                        half = slice(b * C, (b + 1) * C)
                        act.activation(kq[o][half, b, :], mix_bank[half, 0:M], ACT.Copy)
                    act.activation(vt[o][:, :, :].rearrange("m b c -> m (b c)"), mix_bank[:, M:M + 2 * C], ACT.Copy)\
                       .then_inc(s_kqv_sb, 1)
                exps(i, 1)
                if isinstance(i, int) and i == -1:
                    act.wait_ge(s_up, 64)
                    act.activation(up_high[:, :, :], up_raw[:, :, :], ACT.Copy).then_inc(s_up_high, 1)
                if has(i - 2):
                    q = i - 2
                    act.wait_ge(s_x1t, q + 1)
                    act.activation(xt[:, :, pair_rows(q)], x1t_bank[:, :].rearrange("p (t r) -> p t r", t=NT),
                                   ACT.Copy).then_inc(s_x1t_sb, 1)
                    act.wait_ge(s_xn2t, q + 1)
                    if past(q, 2):
                        act.wait_ge(s_stack[s], 32 * (q - s))
                    act.activation(high[s][:, :, :], mix_bank[:, :].rearrange("p (t r) -> p t r", t=NT),
                                   ACT.Copy).then_inc(s_high, 1)

            pipeline(act, step)

            act.wait_ge(s_x1, PAIRS)

            def gelus(c):
                for h in range(HEADS):
                    act.wait_ge(s_upmm, c * HEADS + h + 1)
                    if not isinstance(c, int) or h >= 2 * HPT:
                        act.wait_ge(s_downmm, c * NT + h // HPT - 1)
                    act.activation(hidden[h % (2 * HPT)], up_bank[h % 4][:, :], ACT.Gelu).then_inc(s_gelu, 1)

            gelus(0)
            with act.Fori(1, CHUNKS) as c:
                gelus(c)

        @block.vector
        def _(dve):
            dve.memset(kq[0][0:C, 1, :], 0.0)
            dve.memset(kq[0][C:P, 0, :], 0.0)
            dve.memset(kq[1][0:C, 1, :], 0.0)
            dve.memset(kq[1][C:P, 0, :], 0.0)
            for w in (wkq, wv_raw, ws_raw):
                dve.memset(w[0:C, 1, :], 0.0)
                dve.memset(w[C:P, 0, :], 0.0)
            dve.memset(up_raw[:, :, :], 0.0).then_inc(s_zero, 1)
            dve.wait_ge(s_zero, 1)
            dve.wait_ge(s_tanh, 1)
            dve.wait_ge(s_wvs, 64)
            for to, w in ((wv_sb, wv_raw), (ws_sb, ws_raw)):
                dve.tensor_scalar(to[:, :], w[:, :, :].rearrange("p b c -> p (b c)"), tanh_g[:, 0:1], None, ALU.mult)\
                   .then_inc(s_wvs_sb, 1)

            def maxima(q, h):
                if has(q):
                    dve.wait_ge(s_score, 2 * q + h + 1)
                    dve.tensor_reduce(neg_max[h][:, :], score_bank[h][:, :].rearrange("n (g m) -> n g m", g=4),
                                      AX.X, ALU.max, negate=True).then_inc(s_max, 1)

            def inverses(q, h):
                if has(q):
                    dve.wait_ge(s_exp, 2 * q + h + 1)
                    dve.reciprocal(inv_sum[h][:, :], sums[h][:, :]).then_inc(s_inv, 1)

            def moments(bn, stats, x, done_bn, done, q):
                dve.bn_stats(bn[:, :], x).then_inc(done_bn, 1)
                dve.wait_ge(s_zero, 1)
                dve.wait_ge(done_bn, q + 1)
                dve.bn_aggr(stats[:, :], bn[:, :]).then_inc(done, 1)

            def step(i, s):
                o = 1 - s
                maxima(i, 0)
                store_probs_t(dve, dve.tensor_copy, i - 1, o, 0)
                if has(i + 1):
                    q = i + 1
                    dve.wait_ge(s_xevac, q + 1)
                    if past(q, 2):
                        dve.wait_ge(s_xn, q - 1)
                    moments(bn1, stats1[o], x_rows[:, bass.ds(q, 1), :], s_bn1a, s_st1, q)
                inverses(i, 0)
                maxima(i, 1)
                if has(i + 1):
                    q = i + 1
                    dve.wait_ge(s_rstd1, q + 1)
                    if past(q, 2):
                        dve.wait_ge(s_att, q - 1)
                    dve.tensor_scalar(xn[o][:, :].rearrange("p (a n) -> p a n", a=1), x_rows[:, bass.ds(q, 1), :],
                                      stats1[o][:, 0:1], rstd1[o][:, 0:1], ALU.subtract, ALU.mult).then_inc(s_xn, 1)
                if has(i - 1):
                    q = i - 1
                    dve.wait_ge(s_att, q + 1)
                    if past(q, 2):
                        dve.wait_ge(s_x1t, q - 1)
                        dve.wait_ge(s_xn2, q - 1)
                    dve.tensor_tensor(x1[o][:, :].rearrange("p (a n) -> p a n", a=1), x_rows[:, bass.ds(q, 1), :],
                                      x1_bank[:, :].rearrange("p (a n) -> p a n", a=1), ALU.add).then_inc(s_x1, 1)
                    dve.wait_ge(s_x1, q + 1)
                    moments(bn2, stats2[o], x1[o][:, :], s_bn2a, s_st2, q)
                inverses(i, 1)
                if has(i - 2):
                    q = i - 2
                    dve.wait_ge(s_high, q + 1)
                    dve.tensor_tensor(low[s][:, :, :], mix_bank[:, :].rearrange("p (t r) -> p t r", t=NT),
                                      high[s][:, :, :].bitcast(F32), ALU.subtract).then_inc(s_low, 1)
                if isinstance(i, int) and i == -1:
                    dve.wait_ge(s_up_high, 1)
                    dve.tensor_tensor(up_low[:, :, :], up_raw[:, :, :], up_high[:, :, :].bitcast(F32), ALU.subtract)\
                       .then_inc(s_up_low, 1)
                    dve.wait_ge(s_down, 16)
                    dve.tensor_scalar(down_sb[:, :, :], down_sb[:, :, :], tanh_g[:, 1:2], None, ALU.mult)\
                       .then_inc(s_down_sb, 1)
                    for c in range(CHUNKS):
                        dve.tensor_scalar(out_index[:, c, :], perm_sb[:, :], float(c * N), None, ALU.add)\
                           .then_inc(s_index, 1)

            pipeline(dve, step)

            def results(c):
                for t in range(NT):
                    tile = c * NT + t
                    dve.wait_ge(s_downmm, tile + 1)
                    if not isinstance(c, int):
                        dve.wait_ge(s_out[t % 4], 16 * c)
                    dve.tensor_tensor(result[t % 4].rearrange("p (a r) -> p a r", a=1),
                                      down_bank[t % 2][:, :].rearrange("p (a r) -> p a r", a=1),
                                      xt[:, t:t + 1, bass.ds(c * CH, CH)], ALU.add).then_inc(s_res, 1)

            dve.wait_ge(s_x1t_sb, PAIRS)
            results(0)
            with dve.Fori(1, CHUNKS) as c:
                results(c)


def kernel(x, ctx_1024, g_xattn, g_ffn, L0_xattn_Wq, L0_xattn_Wk, L0_xattn_Wv, L0_xattn_Wskip,
           L0_ffn_up, L0_ffn_down, L0_ffn_perm):
    import numpy as np
    from concourse import bacc
    from concourse.bass_utils import run_bass_kernel_spmd

    batches, channels, n = x.shape
    rows = batches * channels
    head = 512
    xt = np.asarray(x).reshape(rows, n).T
    ins = {
        "x_head": xt[:, :head],
        "x_rest": xt[:, head:],
        "ctx": np.asarray(ctx_1024).reshape(rows, -1),
        "perm": np.asarray(L0_ffn_perm).astype(np.int32).reshape(n // 128, 128).T,
        "gates": np.concatenate([np.asarray(g_xattn), np.asarray(g_ffn)]).reshape(1, 2),
        "wq": L0_xattn_Wq,
        "wk": L0_xattn_Wk,
        "wv_t": np.asarray(L0_xattn_Wv).T,
        "wskip_t": np.asarray(L0_xattn_Wskip).T,
        "up": L0_ffn_up,
        "down": L0_ffn_down,
    }
    nc = bacc.Bacc("TRN2", target_bir_lowering=False, num_devices=1)
    arrays, args = {}, {}
    for name, a in ins.items():
        a = np.ascontiguousarray(a)
        arrays[f"in_{name}"] = a
        args[name] = nc.dram_tensor(f"in_{name}", a.shape, mybir.dt.from_np(a.dtype), kind="ExternalInput").ap()
    chunk = 512
    out = nc.dram_tensor("out_0", (rows // chunk * n, chunk), F32, kind="ExternalOutput").ap()
    build_block(nc, out=out, **args)
    r = run_bass_kernel_spmd(nc, [arrays], core_ids=[0])
    y = r.results[0]["out_0"].reshape(rows // chunk, n, chunk)
    return np.ascontiguousarray(y.transpose(0, 2, 1)).reshape(batches, channels, n)
```

```python
from contextlib import ExitStack

import concourse.bass as bass
from concourse import mybir
from concourse.alu_op_type import AluOpType as ALU

ACT = mybir.ActivationFunctionType
AX = mybir.AxisListType
F32 = mybir.dt.float32
F32R = mybir.dt.float32r
I32 = mybir.dt.int32
U32 = mybir.dt.uint32

EPS = 1e-5


def build_block(nc, x_head, x_rest, ctx, perm, gates, wq, wk, wv_t, wskip_t, up, down, out):
    P = 128
    N, HEAD_ROWS = x_head.shape
    ROWS = HEAD_ROWS + x_rest.shape[1]
    M = ctx.shape[1]
    C = wq.shape[0]
    HEADS, DH, MH = up.shape
    NT = N // P
    PAIRS = ROWS // P
    CH = 512
    CHUNKS = ROWS // CH
    PPC = CH // P
    HPT = P // DH
    UNIT = 2 * 2 * M
    UNSTAGED = 5
    UP_PARTS = 4
    SCALE = 1.0 / float(C) ** 0.5

    es = ExitStack()

    def sb(name, shape, dt=F32):
        return es.enter_context(nc.sbuf_tensor(name, shape, dt))

    def sem(name):
        return es.enter_context(nc.semaphore(name))

    with es:
        xt = sb("xt", [P, NT, ROWS])
        x_rows = sb("x_rows", [P, PAIRS, N])
        stack = sb("stack", [P, 2 * NT, ROWS], F32R)
        x_stage = [sb(f"x_stage{s}", [P, NT, P]) for s in range(2)]
        ctx_stage = [sb(f"ctx_stage{s}", [P, M]) for s in range(2)]
        xn = [sb(f"xn{s}", [P, N]) for s in range(2)]
        x1 = [sb(f"x1_{s}", [P, N]) for s in range(2)]
        xn2 = [sb(f"xn2_{s}", [P, N]) for s in range(2)]
        kq = [sb(f"kq{s}", [P, 2, M]) for s in range(2)]
        vt = [sb(f"vt{s}", [P, 2, C]) for s in range(2)]
        probs = [sb(f"probs{h}", [P, 4, M]) for h in range(2)]
        pn = [[sb(f"pn{s}_{h}", [P, 4, M]) for h in range(2)] for s in range(2)]
        probs_t = [sb(f"probs_t{s}", [P, 2, NT, P]) for s in range(2)]
        high = [sb(f"high{s}", [P, NT, P], F32R) for s in range(2)]
        low = [sb(f"low{s}", [P, NT, P], F32R) for s in range(2)]
        neg_max = [sb(f"neg_max{h}", [P, 4]) for h in range(2)]
        sums = [sb(f"sums{h}", [P, 4]) for h in range(2)]
        inv_sum = [sb(f"inv_sum{h}", [P, 4]) for h in range(2)]
        bn1 = sb("bn1", [P, 6])
        bn2 = sb("bn2", [P, 6])
        stats1 = [sb(f"stats1_{s}", [P, 2]) for s in range(2)]
        stats2 = [sb(f"stats2_{s}", [P, 2]) for s in range(2)]
        var1 = sb("var1", [P, 1])
        var2 = sb("var2", [P, 1])
        rstd1 = [sb(f"rstd1_{s}", [P, 1]) for s in range(2)]
        rstd2 = [sb(f"rstd2_{s}", [P, 1]) for s in range(2)]
        minus_half = sb("minus_half", [P, 1])
        minus_one = sb("minus_one", [P, 1])
        eps = sb("eps", [P, 1])
        neg_mean2 = [sb(f"neg_mean2_{s}", [P, 1]) for s in range(2)]
        ident = sb("ident", [P, P])
        perm_sb = sb("perm_sb", [P, NT], I32)
        out_index = sb("out_index", [P, CHUNKS, NT], I32)
        gates_sb = sb("gates_sb", [P, 2])
        tanh_g = sb("tanh_g", [P, 2])
        wq_sb = sb("wq_sb", [C, C])
        wk_sb = sb("wk_sb", [C, 2, C])
        wkq = sb("wkq", [P, 2, C])
        wv_raw = sb("wv_raw", [P, 2, C])
        wv_sb = sb("wv_sb", [P, 2 * C])
        ws_raw = sb("ws_raw", [P, 2, C])
        ws_sb = sb("ws_sb", [P, 2 * C])
        up_raw = sb("up_raw", [P, HEADS, MH])
        up_high = sb("up_high", [P, HEADS, MH], F32R)
        up_low = sb("up_low", [P, HEADS, MH], F32R)
        down_sb = sb("down_sb", [P, HEADS, DH])
        x_flat = x_rows[:, :, :].rearrange("p a n -> p (a n)")
        hidden = [x_flat[:, g * CH:(g + 1) * CH] for g in range(2 * HPT)]
        result = [x_flat[:, (2 * HPT + g) * CH:(2 * HPT + g + 1) * CH] for g in range(4)]

        bank = [es.enter_context(nc.psum_tensor(f"bank{b}", [P, 512], F32)) for b in range(8)]
        score_bank = bank[0:2]
        probs_t_bank = bank[2:4]
        x1_bank, x_bank, kqv_bank, xn2_bank = bank[4:8]
        up_bank = bank[0:4]
        down_bank = [x1_bank, x_bank]

        s_perm = sem("perm_loaded")
        s_wkq = sem("wkq_loaded")
        s_gates = sem("gates_loaded")
        s_wvs = sem("wv_wskip_loaded")
        s_up = sem("up_loaded")
        s_down = sem("down_loaded")
        s_zero = sem("dve_zeroed")
        s_ident = sem("identity_made")
        s_half = sem("constants_set")
        s_index = sem("index_made")
        s_tanh = sem("tanh_made")
        s_wkq_mm = sem("wkq_multiplied")
        s_wkq_sb = sem("wkq_ready")
        s_wvs_sb = sem("wv_wskip_ready")
        s_up_high = sem("up_high_ready")
        s_up_low = sem("up_low_ready")
        s_down_sb = sem("down_ready")
        s_head = sem("x_head_gathered")
        s_rest = sem("x_rest_gathered")
        s_xstage = [sem(f"x_staged{s}") for s in range(2)]
        s_cstage = [sem(f"ctx_staged{s}") for s in range(2)]
        s_t0 = sem("x_transposed")
        s_xevac = sem("x_rows_stored")
        s_bn1a = sem("bn1_done")
        s_st1 = sem("stats1_done")
        s_var1 = sem("var1_done")
        s_rstd1 = sem("rstd1_done")
        s_xn = sem("xn_ready")
        s_kqv = sem("kq_v_multiplied")
        s_kq_sb = sem("kq_stored")
        s_vt_sb = sem("v_stored")
        s_score = sem("scores_ready")
        s_max = sem("max_ready")
        s_exp = sem("exp_done")
        s_inv = sem("inv_sum_ready")
        s_pn = sem("probs_normalised")
        s_pt = sem("probs_transposed")
        s_pt_sb = [sem(f"probs_t_stored{h}") for h in range(2)]
        s_skip = sem("skip_done")
        s_att = sem("attention_done")
        s_x1 = sem("x1_ready")
        s_bn2a = sem("bn2_done")
        s_st2 = sem("stats2_done")
        s_var2 = sem("var2_done")
        s_neg = sem("neg_mean2_ready")
        s_rstd2 = sem("rstd2_ready")
        s_xn2 = sem("xn2_ready")
        s_x1t = sem("x1_transposed")
        s_x1t_sb = sem("x1_t_stored")
        s_xn2t = sem("xn2_transposed")
        s_high = sem("high_ready")
        s_low = sem("low_ready")
        s_stack = [sem(f"stacked{s}") for s in range(2)]
        s_upmm = sem("up_multiplied")
        s_gelu = sem("gelu_done")
        s_downmm = sem("down_multiplied")
        s_res = sem("result_ready")
        s_out = [sem(f"result_stored{g}") for g in range(4)]

        block = es.enter_context(nc.Block())

        def pipeline(engine, step):
            for i in range(-1, 4):
                step(i, i % 2)
            with engine.Fori(2, PAIRS // 2 - 1) as k:
                for s in range(2):
                    step(2 * k + s, s)
            for i in range(PAIRS - 2, PAIRS + 3):
                step(i, i % 2)

        def has(q):
            return not isinstance(q, int) or 0 <= q < PAIRS

        def past(q, least):
            return not isinstance(q, int) or q >= least

        def pair_rows(q):
            return bass.ds(q * P, P)

        def staged(q, s, first=0):
            return 8 * (q - s - first) + 16

        def store_probs_t(engine, copy, q, s, h):
            if has(q):
                engine.wait_ge(s_pt, 2 * q + h + 1)
                if past(q, 2):
                    engine.wait_ge(s_att, q - 1)
                copy(probs_t[s][:, :, 2 * h:2 * h + 2, :].rearrange("m b t n -> m b (t n)"),
                     probs_t_bank[h][:, :].rearrange("m (b n) -> m b n", b=2)).then_inc(s_pt_sb[h], 1)

        @block.sync
        def _(sp):
            sp.dma_start(perm_sb[:, :], perm).then_inc(s_perm, 16)
            sp.dma_start(wq_sb[:, :], wq).then_inc(s_wkq, 16)
            sp.dma_start(gates_sb[:, :], gates.to_broadcast([P, 2])).then_inc(s_gates, 16)

            def stage(q, s):
                if has(q):
                    if past(q, UNSTAGED):
                        if past(q, UNSTAGED + 2):
                            sp.wait_ge(s_t0, q - 1)
                        sp.wait_ge(s_rest, 16 * NT)
                        sp.dma_start(x_stage[s][:, :, :], xt[:, :, pair_rows(q)]).then_inc(s_xstage[s], 16)
                    if past(q, 2):
                        sp.wait_ge(s_kqv, q - 1)
                    sp.dma_start(ctx_stage[s][:, :], ctx[pair_rows(q), :]).then_inc(s_cstage[s], 16)

            def step(i, s):
                if isinstance(i, int) and i == -1:
                    stage(0, 0)
                    for b in range(2):
                        half = slice(b * C, (b + 1) * C)
                        sp.dma_start(wv_raw[half, b, :], wv_t).then_inc(s_wvs, 16)
                        sp.dma_start(ws_raw[half, b, :], wskip_t).then_inc(s_wvs, 16)
                    stage(1, 1)
                    sp.wait_ge(s_zero, 1)
                    for b in range(2):
                        for r in range(2):
                            rows = slice(b * 2 * DH + r * DH, b * 2 * DH + (r + 1) * DH)
                            sp.dma_start(up_raw[rows, r::2, :], up[r::2, :, :].rearrange("h d m -> d h m"))\
                              .then_inc(s_up, 16)
                    sp.dma_start(down_sb[:, :, :], down.rearrange("h m d -> m h d")).then_inc(s_down, 16)
                    return
                stage(i + 2, s)
                if has(i - 3):
                    q = i - 3
                    sp.wait_ge(s_low, q + 1)
                    lo, hi = slice(0, 2 * DH), slice(2 * DH, P)
                    for dst, src, first in ((lo, (high, lo), 0), (hi, (low, lo), 0),
                                            (lo, (high, hi), 1), (hi, (low, hi), 1)):
                        part, rows = src
                        sp.dma_start(stack[dst, first::2, pair_rows(q)].bitcast(F32),
                                     part[1 - s][rows, :, :].bitcast(F32)).then_inc(s_stack[1 - s], 16)

            pipeline(sp, step)

        @block.gpsimd
        def _(pool):
            pool.memset(ident[:, :], 0.0).then_inc(s_ident, 1)
            pool.memset(minus_half[:, :], -0.5).then_inc(s_half, 1)
            pool.memset(minus_one[:, :], -1.0).then_inc(s_half, 1)
            pool.memset(eps[:, :], EPS).then_inc(s_half, 1)
            pool.wait_ge(s_ident, 1)
            pool.affine_select(out=ident[:, :], in_=ident[:, :], compare_op=ALU.not_equal, fill=1.0,
                               base=0, pattern=[[-1, P]], channel_multiplier=1).then_inc(s_ident, 1)
            pool.wait_ge(s_perm, 16)
            for t in range(NT):
                pool.indirect_dma_start(
                    xt[:, t, 0:HEAD_ROWS], None, x_head,
                    bass.IndirectOffsetOnAxis(ap=perm_sb[:, t:t + 1].bitcast(U32), axis=0)).then_inc(s_head, 16)
            for t in range(NT):
                pool.indirect_dma_start(
                    xt[:, t, HEAD_ROWS:ROWS], None, x_rest,
                    bass.IndirectOffsetOnAxis(ap=perm_sb[:, t:t + 1].bitcast(U32), axis=0)).then_inc(s_rest, 16)
            pool.wait_ge(s_half, 3)

            def rstd(var, stats, to, done_var, done, q):
                pool.tensor_tensor(var[:, :], stats[:, 1:2], eps[:, :], ALU.add).then_inc(done_var, 1)
                pool.wait_ge(done_var, q + 1)
                pool.tensor_tensor(to[:, :], var[:, :], minus_half[:, :], ALU.pow).then_inc(done, 1)

            def normalise(q, s, h):
                if has(q):
                    pool.wait_ge(s_inv, 2 * q + h + 1)
                    if past(q, 2):
                        pool.wait_ge(s_pt, 2 * q + h - 3)
                    pool.tensor_tensor(pn[s][h][:, :, :], probs[h][:, :, :],
                                       inv_sum[h][:, :].unsqueeze(2).to_broadcast([P, 4, M]),
                                       ALU.mult).then_inc(s_pn, 1)

            def step(i, s):
                if has(i - 2):
                    q = i - 2
                    pool.wait_ge(s_st2, q + 1)
                    if past(q, 2):
                        pool.wait_ge(s_xn2t, q - 1)
                    pool.tensor_tensor(neg_mean2[s][:, :], stats2[s][:, 0:1], minus_one[:, :], ALU.mult).then_inc(s_neg, 1)
                    rstd(var2, stats2[s], rstd2[s], s_var2, s_rstd2, q)
                    pool.wait_ge(s_half, 3)
                    pool.wait_ge(s_rstd2, q + 1)
                    pool.wait_ge(s_neg, q + 1)
                    pool.tensor_scalar(xn2[s][:, :], x1[s][:, :], neg_mean2[s][:, 0:1], rstd2[s][:, 0:1],
                                       ALU.add, ALU.mult).then_inc(s_xn2, 1)
                if has(i + 1):
                    q, o = i + 1, 1 - s
                    pool.wait_ge(s_st1, q + 1)
                    rstd(var1, stats1[o], rstd1[o], s_var1, s_rstd1, q)
                normalise(i, s, 0)
                normalise(i, s, 1)

            pipeline(pool, step)

            pool.wait_ge(s_index, CHUNKS)
            for c in range(CHUNKS):
                for t in range(NT):
                    tile = c * NT + t
                    pool.wait_ge(s_res, tile + 1)
                    pool.indirect_dma_start(
                        out, bass.IndirectOffsetOnAxis(ap=out_index[:, c, t:t + 1].bitcast(U32), axis=0),
                        result[tile % 4], None).then_inc(s_out[tile % 4], 16)
            for g in range(4):
                pool.wait_ge(s_out[g], 16 * CHUNKS * NT // 4)

        @block.tensor
        def _(pe):
            pe.wait_ge(s_ident, 2)
            pe.wait_ge(s_wkq, 48)
            pe.matmul(kqv_bank[:, 0:C], wk_sb[:, :, :].rearrange("o b c -> o (b c)"), wq_sb[:, :],
                      start=True, stop=True).then_inc(s_wkq_mm, 1)

            def transposes(to, of, cols=P):
                for t in range(NT):
                    last = pe.transpose(to[:, t * P:(t + 1) * P], of(t), ident[:, :])
                return last

            def scores(q, s, h):
                if has(q):
                    if h == 0:
                        if not past(q, 1):
                            pe.wait_ge(s_zero, 1)
                        pe.wait_ge(s_xn, q + 1)
                        pe.wait_ge(s_kq_sb, 2 * q + 2)
                    if past(q, 1):
                        pe.wait_ge(s_exp, 2 * q + h - 1)
                    for j in range(2):
                        t = 2 * h + j
                        last = pe.matmul(score_bank[h][:, j * 2 * M:(j + 1) * 2 * M], xn[s][:, t * P:(t + 1) * P],
                                         kq[s][:, :, :].rearrange("c b m -> c (b m)"), start=True, stop=True)
                    last.then_inc(s_score, 1)

            def probs_transposes(q, s, h):
                if has(q):
                    pe.wait_ge(s_pn, 2 * q + h + 1)
                    if past(q, 1):
                        pe.wait_ge(s_pt_sb[h], q)
                    for j in range(2):
                        for b in range(2):
                            at = (2 * b + j) * P
                            last = pe.transpose(probs_t_bank[h][:, at:at + P], pn[s][h][:, 2 * j + b, :], ident[:, :])
                    last.then_inc(s_pt, 1)

            def step(i, s):
                o = 1 - s
                scores(i, s, 0)
                if has(i + 1):
                    q = i + 1
                    if past(q, 4):
                        pe.wait_ge(s_x1t_sb, q - 3)
                    elif past(q, 1):
                        pe.wait_ge(s_xevac, q)
                    if past(q, UNSTAGED):
                        pe.wait_ge(s_xstage[o], staged(q, 1 - o, UNSTAGED))
                        transposes(x_bank, lambda t: x_stage[o][:, t, :]).then_inc(s_t0, 1)
                    else:
                        pe.wait_ge(s_head if q < PPC else s_rest, 16 * NT)
                        transposes(x_bank, lambda t: xt[:, t, q * P:(q + 1) * P]).then_inc(s_t0, 1)
                probs_transposes(i - 1, o, 0)
                probs_transposes(i - 1, o, 1)
                if has(i - 2):
                    q = i - 2
                    pe.wait_ge(s_x1, q + 1)
                    if has(q + 3):
                        pe.wait_ge(s_xevac, q + 4)
                    else:
                        pe.wait_ge(s_x1t_sb, q)
                    transposes(x_bank, lambda t: x1[s][:, t * P:(t + 1) * P]).then_inc(s_x1t, 1)
                scores(i, s, 1)
                if has(i - 1):
                    if past(i - 1, 1):
                        pe.wait_ge(s_x1, i - 1)
                    pe.matmul(x1_bank[:, :], ws_sb[:, :], xn[o][:, :], start=True, stop=False,
                              skip_group_check=True).then_inc(s_skip, 1)
                if has(i + 1):
                    q = i + 1
                    pe.wait_ge(s_cstage[o], staged(q, o))
                    if past(q, 1):
                        pe.wait_ge(s_kq_sb, 2 * q)
                        pe.wait_ge(s_vt_sb, q)
                    else:
                        pe.wait_ge(s_wkq_sb, 2)
                        pe.wait_ge(s_wvs_sb, 2)
                    pe.matmul(kqv_bank[:, 0:M], wkq[:, :, :].rearrange("c b e -> c (b e)"), ctx_stage[o][:, :],
                              start=True, stop=True)
                    pe.matmul(kqv_bank[:, M:M + 2 * C], ctx_stage[o][:, :], wv_sb[:, :],
                              start=True, stop=True).then_inc(s_kqv, 1)
                if has(i - 1):
                    q = i - 1
                    pe.wait_ge(s_vt_sb, q + 1)
                    pe.wait_ge(s_pt_sb[0], q + 1)
                    pe.wait_ge(s_pt_sb[1], q + 1)
                    for b in range(2):
                        last = pe.matmul(x1_bank[b * C:(b + 1) * C, :], vt[o][:, b, :],
                                         probs_t[o][:, b, :, :].rearrange("m t n -> m (t n)"),
                                         start=False, stop=True, skip_group_check=True)
                    last.then_inc(s_att, 1)
                if has(i - 2):
                    q = i - 2
                    pe.wait_ge(s_xn2, q + 1)
                    if past(q, 1):
                        pe.wait_ge(s_low, q)
                    transposes(xn2_bank, lambda t: xn2[s][:, t * P:(t + 1) * P]).then_inc(s_xn2t, 1)

            pipeline(pe, step)

            def up_tile(c, t):
                for h in range(t * HPT, (t + 1) * HPT):
                    if not isinstance(c, int) or c > 0 or h >= 4:
                        pe.wait_ge(s_gelu, c * HEADS + h - 3)
                    part = 2 * t + (h % HPT) // 2
                    for w, first in ((up_high, True), (up_low, False)):
                        last = pe.matmul(up_bank[h % 4][:, :], w[:, h, :], stack[:, part, bass.ds(c * CH, CH)],
                                         start=first, stop=not first)
                    last.then_inc(s_upmm, 1)

            def down_tile(c, t):
                pe.wait_ge(s_gelu, c * HEADS + (t + 1) * HPT)
                if not isinstance(c, int) or c > 0 or t >= 2:
                    pe.wait_ge(s_res, c * NT + t - 1)
                for g in range(HPT):
                    h = t * HPT + g
                    last = pe.matmul(down_bank[t % 2][g * DH:(g + 1) * DH, :], down_sb[:, h, :], hidden[h % (2 * HPT)],
                                     start=True, stop=True, skip_group_check=True)
                last.then_inc(s_downmm, 1)

            def chunk(c, last):
                for t in range(NT):
                    if t + 1 < NT:
                        up_tile(c, t + 1)
                    elif not last:
                        stacked(c + 1)
                        up_tile(c + 1, 0)
                    down_tile(c, t)

            def stacked(c):
                for s in range(2):
                    pe.wait_ge(s_stack[s], (c + 1) * (PPC // 2 * 4 * 16))

            pe.wait_ge(s_exp, 2 * PAIRS)
            pe.wait_ge(s_pt_sb[0], PAIRS)
            pe.wait_ge(s_pt_sb[1], PAIRS)
            pe.wait_ge(s_up_high, UP_PARTS)
            pe.wait_ge(s_up_low, UP_PARTS)
            stacked(0)
            up_tile(0, 0)
            pe.wait_ge(s_x1, PAIRS)
            pe.wait_ge(s_x1t_sb, PAIRS)
            pe.wait_ge(s_down_sb, 1)
            chunk(0, False)
            with pe.Fori(1, CHUNKS - 1) as c:
                chunk(c, False)
            chunk(CHUNKS - 1, True)

        @block.scalar
        def _(act):
            for b in range(2):
                act.dma_start(wk_sb[:, b, :], wk).then_inc(s_wkq, 16)
            act.wait_ge(s_gates, 16)
            act.activation(tanh_g[:, :], gates_sb[:, :], ACT.Tanh).then_inc(s_tanh, 1)
            act.wait_ge(s_wkq_mm, 1)
            act.activation(wkq[0:C, 0, :], kqv_bank[0:C, 0:C], ACT.Copy, scale=SCALE).then_inc(s_wkq_sb, 1)
            act.activation(wkq[C:P, 1, :], kqv_bank[C:P, 0:C], ACT.Copy, scale=SCALE).then_inc(s_wkq_sb, 1)

            def exps(q, h):
                if has(q):
                    act.wait_ge(s_max, 2 * q + h + 1)
                    if past(q, 1):
                        act.wait_ge(s_pn, 2 * q + h - 1)
                    for g in range(4):
                        last = act.activation(probs[h][:, g, :], score_bank[h][:, g * M:(g + 1) * M], ACT.Exp,
                                              bias=neg_max[h][:, g:g + 1], accum_out=sums[h][:, g:g + 1])
                    last.then_inc(s_exp, 1)

            def step(i, s):
                o = 1 - s
                if has(i + 1):
                    act.wait_ge(s_t0, i + 2)
                    act.activation(x_rows[:, bass.ds(i + 1, 1), :],
                                   x_bank[:, :].rearrange("p (a n) -> p a n", a=1), ACT.Copy).then_inc(s_xevac, 1)
                exps(i, 0)
                store_probs_t(act, act.copy, i - 1, o, 1)
                if has(i - 2):
                    q = i - 2
                    act.wait_ge(s_x1t, q + 1)
                    act.activation(xt[:, :, pair_rows(q)], x_bank[:, :].rearrange("p (t r) -> p t r", t=NT),
                                   ACT.Copy).then_inc(s_x1t_sb, 1)
                if has(i + 1):
                    q = i + 1
                    act.wait_ge(s_kqv, q + 1)
                    if past(q, 2):
                        act.wait_ge(s_score, 2 * q - 2)
                    for b in range(2):
                        half = slice(b * C, (b + 1) * C)
                        act.activation(kq[o][half, b, :], kqv_bank[half, 0:M], ACT.Copy).then_inc(s_kq_sb, 1)
                exps(i, 1)
                if has(i + 1):
                    q = i + 1
                    if past(q, 2):
                        act.wait_ge(s_att, q - 1)
                    act.activation(vt[o][:, :, :].rearrange("m b c -> m (b c)"), kqv_bank[:, M:M + 2 * C], ACT.Copy)\
                       .then_inc(s_vt_sb, 1)
                if isinstance(i, int) and 0 <= i < UP_PARTS:
                    part = slice(i * HEADS // UP_PARTS, (i + 1) * HEADS // UP_PARTS)
                    act.wait_ge(s_up, 64)
                    act.activation(up_high[:, part, :], up_raw[:, part, :], ACT.Copy).then_inc(s_up_high, 1)
                if has(i - 2):
                    q = i - 2
                    act.wait_ge(s_xn2t, q + 1)
                    if past(q, 2):
                        act.wait_ge(s_stack[s], 32 * (q - s))
                    act.activation(high[s][:, :, :], xn2_bank[:, :].rearrange("p (t r) -> p t r", t=NT),
                                   ACT.Copy).then_inc(s_high, 1)

            pipeline(act, step)

            act.wait_ge(s_x1, PAIRS)

            def gelus(c):
                for h in range(HEADS):
                    act.wait_ge(s_upmm, c * HEADS + h + 1)
                    if not isinstance(c, int) or h >= 2 * HPT:
                        act.wait_ge(s_downmm, c * NT + h // HPT - 1)
                    act.activation(hidden[h % (2 * HPT)], up_bank[h % 4][:, :], ACT.Gelu).then_inc(s_gelu, 1)

            gelus(0)
            with act.Fori(1, CHUNKS) as c:
                gelus(c)

        @block.vector
        def _(dve):
            dve.memset(kq[0][0:C, 1, :], 0.0)
            dve.memset(kq[0][C:P, 0, :], 0.0)
            dve.memset(kq[1][0:C, 1, :], 0.0)
            dve.memset(kq[1][C:P, 0, :], 0.0)
            for w in (wkq, wv_raw, ws_raw):
                dve.memset(w[0:C, 1, :], 0.0)
                dve.memset(w[C:P, 0, :], 0.0)
            dve.memset(up_raw[:, :, :], 0.0).then_inc(s_zero, 1)
            dve.wait_ge(s_zero, 1)
            dve.wait_ge(s_tanh, 1)
            dve.wait_ge(s_wvs, 64)
            for to, w in ((wv_sb, wv_raw), (ws_sb, ws_raw)):
                dve.tensor_scalar(to[:, :], w[:, :, :].rearrange("p b c -> p (b c)"), tanh_g[:, 0:1], None, ALU.mult)\
                   .then_inc(s_wvs_sb, 1)

            def maxima(q, h):
                if has(q):
                    dve.wait_ge(s_score, 2 * q + h + 1)
                    dve.tensor_reduce(neg_max[h][:, :], score_bank[h][:, :].rearrange("n (g m) -> n g m", g=4),
                                      AX.X, ALU.max, negate=True).then_inc(s_max, 1)

            def inverses(q, h):
                if has(q):
                    dve.wait_ge(s_exp, 2 * q + h + 1)
                    dve.reciprocal(inv_sum[h][:, :], sums[h][:, :]).then_inc(s_inv, 1)

            def aggregate(bn, stats, done_bn, done, q):
                dve.wait_ge(s_zero, 1)
                dve.wait_ge(done_bn, q + 1)
                dve.bn_aggr(stats[:, :], bn[:, :]).then_inc(done, 1)

            def step(i, s):
                o = 1 - s
                if has(i - 2):
                    dve.wait_ge(s_x1, i - 1)
                    if past(i - 2, 1):
                        dve.wait_ge(s_st2, i - 2)
                    dve.bn_stats(bn2[:, :], x1[s][:, :]).then_inc(s_bn2a, 1)
                maxima(i, 0)
                if has(i - 2):
                    aggregate(bn2, stats2[s], s_bn2a, s_st2, i - 2)
                if has(i + 1):
                    q = i + 1
                    dve.wait_ge(s_xevac, q + 1)
                    if past(q, 1):
                        dve.wait_ge(s_st1, q)
                    if past(q, 2):
                        dve.wait_ge(s_xn, q - 1)
                    dve.bn_stats(bn1[:, :], x_rows[:, bass.ds(q, 1), :]).then_inc(s_bn1a, 1)
                store_probs_t(dve, dve.tensor_copy, i - 1, o, 0)
                if has(i + 1):
                    aggregate(bn1, stats1[o], s_bn1a, s_st1, q)
                maxima(i, 1)
                inverses(i, 0)
                if has(i - 3):
                    q = i - 3
                    dve.wait_ge(s_high, q + 1)
                    dve.tensor_tensor(low[o][:, :, :], xn2_bank[:, :].rearrange("p (t r) -> p t r", t=NT),
                                      high[o][:, :, :].bitcast(F32), ALU.subtract).then_inc(s_low, 1)
                if has(i + 1):
                    q = i + 1
                    dve.wait_ge(s_rstd1, q + 1)
                    if past(q, 2):
                        dve.wait_ge(s_skip, q - 1)
                    dve.tensor_scalar(xn[o][:, :].rearrange("p (a n) -> p a n", a=1), x_rows[:, bass.ds(q, 1), :],
                                      stats1[o][:, 0:1], rstd1[o][:, 0:1], ALU.subtract, ALU.mult).then_inc(s_xn, 1)
                inverses(i, 1)
                if has(i - 1):
                    q = i - 1
                    dve.wait_ge(s_att, q + 1)
                    if past(q, 2):
                        dve.wait_ge(s_x1t, q - 1)
                        dve.wait_ge(s_xn2, q - 1)
                    dve.tensor_tensor(x1[o][:, :].rearrange("p (a n) -> p a n", a=1), x_rows[:, bass.ds(q, 1), :],
                                      x1_bank[:, :].rearrange("p (a n) -> p a n", a=1), ALU.add).then_inc(s_x1, 1)
                if isinstance(i, int) and 0 <= i < UP_PARTS:
                    part = slice(i * HEADS // UP_PARTS, (i + 1) * HEADS // UP_PARTS)
                    dve.wait_ge(s_up_high, i + 1)
                    dve.tensor_tensor(up_low[:, part, :], up_raw[:, part, :], up_high[:, part, :].bitcast(F32),
                                      ALU.subtract).then_inc(s_up_low, 1)
                if isinstance(i, int) and i == 1:
                    dve.wait_ge(s_down, 16)
                    dve.tensor_scalar(down_sb[:, :, :], down_sb[:, :, :], tanh_g[:, 1:2], None, ALU.mult)\
                       .then_inc(s_down_sb, 1)
                    for c in range(CHUNKS):
                        dve.tensor_scalar(out_index[:, c, :], perm_sb[:, :], float(c * N), None, ALU.add)\
                           .then_inc(s_index, 1)

            pipeline(dve, step)

            def results(c):
                for t in range(NT):
                    tile = c * NT + t
                    dve.wait_ge(s_downmm, tile + 1)
                    if not isinstance(c, int):
                        dve.wait_ge(s_out[t % 4], 16 * c)
                    dve.tensor_tensor(result[t % 4].rearrange("p (a r) -> p a r", a=1),
                                      down_bank[t % 2][:, :].rearrange("p (a r) -> p a r", a=1),
                                      xt[:, t:t + 1, bass.ds(c * CH, CH)], ALU.add).then_inc(s_res, 1)

            dve.wait_ge(s_x1t_sb, PAIRS)
            results(0)
            with dve.Fori(1, CHUNKS) as c:
                results(c)


def kernel(x, ctx_1024, g_xattn, g_ffn, L0_xattn_Wq, L0_xattn_Wk, L0_xattn_Wv, L0_xattn_Wskip,
           L0_ffn_up, L0_ffn_down, L0_ffn_perm):
    import numpy as np
    from concourse import bacc
    from concourse.bass_utils import run_bass_kernel_spmd

    batches, channels, n = x.shape
    rows = batches * channels
    head = 512
    xt = np.asarray(x).reshape(rows, n).T
    ins = {
        "x_head": xt[:, :head],
        "x_rest": xt[:, head:],
        "ctx": np.asarray(ctx_1024).reshape(rows, -1),
        "perm": np.asarray(L0_ffn_perm).astype(np.int32).reshape(n // 128, 128).T,
        "gates": np.concatenate([np.asarray(g_xattn), np.asarray(g_ffn)]).reshape(1, 2),
        "wq": L0_xattn_Wq,
        "wk": L0_xattn_Wk,
        "wv_t": np.asarray(L0_xattn_Wv).T,
        "wskip_t": np.asarray(L0_xattn_Wskip).T,
        "up": L0_ffn_up,
        "down": L0_ffn_down,
    }
    nc = bacc.Bacc("TRN2", target_bir_lowering=False, num_devices=1)
    arrays, args = {}, {}
    for name, a in ins.items():
        a = np.ascontiguousarray(a)
        arrays[f"in_{name}"] = a
        args[name] = nc.dram_tensor(f"in_{name}", a.shape, mybir.dt.from_np(a.dtype), kind="ExternalInput").ap()
    chunk = 512
    out = nc.dram_tensor("out_0", (rows // chunk * n, chunk), F32, kind="ExternalOutput").ap()
    build_block(nc, out=out, **args)
    r = run_bass_kernel_spmd(nc, [arrays], core_ids=[0])
    y = r.results[0]["out_0"].reshape(rows // chunk, n, chunk)
    return np.ascontiguousarray(y.transpose(0, 2, 1)).reshape(batches, channels, n)
```

```python
from contextlib import ExitStack

import concourse.bass as bass
from concourse import mybir
from concourse.alu_op_type import AluOpType as ALU

ACT = mybir.ActivationFunctionType
AX = mybir.AxisListType
F32 = mybir.dt.float32
F32R = mybir.dt.float32r
I32 = mybir.dt.int32
U32 = mybir.dt.uint32

EPS = 1e-5


def build_block(nc, x_head, x_rest, ctx, perm, gates, wq, wk, wv_t, wskip_t, up, down, out):
    P = 128
    N, HEAD_ROWS = x_head.shape
    ROWS = HEAD_ROWS + x_rest.shape[1]
    M = ctx.shape[1]
    C = wq.shape[0]
    HEADS, MH, DH = down.shape
    NT = N // P
    UNITS = HEADS // 2
    PAIRS = ROWS // P
    CH = 512
    CHUNKS = ROWS // CH
    PPC = CH // P
    HPT = P // DH
    PARTS = 4
    K_UP = PARTS * DH
    LATE = 2
    UNSTAGED = 6
    WARM_UP = 8
    SCALE = 1.0 / float(C) ** 0.5

    es = ExitStack()

    def sb(name, shape, dt=F32):
        return es.enter_context(nc.sbuf_tensor(name, shape, dt))

    def sem(name):
        return es.enter_context(nc.semaphore(name))

    with es:
        xt = sb("xt", [P, NT, ROWS])
        x_rows = sb("x_rows", [P, 4, N])
        stack_pairs = PAIRS - LATE
        with ExitStack() as below:
            def sb_below(name, shape):
                return below.enter_context(nc.sbuf_tensor(name, shape, F32))

            raw_floats = HPT * NT * MH + 7 * C
            sb_below("first_pairs", [P, HPT * stack_pairs * N - raw_floats])
            up_raw = sb_below("up_raw", [K_UP, HPT, NT * MH])
            wv_raw = sb_below("wv_raw", [P, 2, C])
            ws_raw = sb_below("ws_raw", [P, 2, C])
            wk_sb = sb_below("wk_sb", [C, 2, C])
            wq_sb = sb_below("wq_sb", [C, C])
        stack = sb("stack", [P, HPT, stack_pairs, N], F32R)
        with ExitStack() as below:
            probs = [sb_below(f"probs{h}", [P, 4, M]) for h in range(2)]
            pn = [sb_below(f"pn{h}", [P, 4, M]) for h in range(2)]
            probs_t = [sb_below(f"probs_t{s}", [P, 2, NT, P]) for s in range(2)]
        late = sb("late", [P, HPT, LATE, N], F32R)
        x_stage = sb("x_stage", [P, 2, N])
        ctx_stage = [sb(f"ctx_stage{s}", [P, M]) for s in range(2)]
        xn_both = sb("xn", [P, 2, N])
        xn = [xn_both[:, s, :] for s in range(2)]
        x1 = [sb(f"x1_{s}", [P, N]) for s in range(2)]
        xn2 = sb("xn2", [P, N])
        kq = [sb(f"kq{s}", [P, 2, M]) for s in range(2)]
        vt = [sb(f"vt{s}", [P, 2, C]) for s in range(2)]
        high = [sb(f"high{s}", [P, NT, P], F32R) for s in range(2)]
        low = [sb(f"low{s}", [P, NT, P], F32R) for s in range(2)]
        neg_max = [sb(f"neg_max{h}", [P, 4]) for h in range(2)]
        sums = [sb(f"sums{h}", [P, 4]) for h in range(2)]
        inv_sum = [sb(f"inv_sum{h}", [P, 4]) for h in range(2)]
        bn1 = sb("bn1", [P, 6])
        bn2 = sb("bn2", [P, 6])
        stats1 = [sb(f"stats1_{s}", [P, 2]) for s in range(2)]
        stats2 = [sb(f"stats2_{s}", [P, 2]) for s in range(2)]
        var1 = sb("var1", [P, 1])
        var2 = sb("var2", [P, 1])
        rstd1 = [sb(f"rstd1_{s}", [P, 1]) for s in range(2)]
        rstd2 = [sb(f"rstd2_{s}", [P, 1]) for s in range(2)]
        minus_half = sb("minus_half", [P, 1])
        minus_one = sb("minus_one", [P, 1])
        eps = sb("eps", [P, 1])
        neg_mean2 = [sb(f"neg_mean2_{s}", [P, 1]) for s in range(2)]
        ident = sb("ident", [P, P])
        perm_sb = sb("perm_sb", [P, NT], I32)
        out_index = sb("out_index", [P, CHUNKS, NT], I32)
        gates_sb = sb("gates_sb", [P, 2])
        tanh_g = sb("tanh_g", [P, 2])
        wkq = sb("wkq", [P, 2, C])
        wv_sb = sb("wv_sb", [P, 2 * C])
        ws_sb = sb("ws_sb", [P, 2 * C])
        up_w = sb("up_w", [K_UP, HPT, NT * MH], F32R)
        down_sb = sb("down_sb", [P, HEADS, DH])

        hidden = [x_stage[:, :, :], x_rows[:, 0:2, :], xn_both[:, :, :], x_rows[:, 2:4, :]]

        wide = [es.enter_context(nc.psum_tensor(f"wide{b}", [P, 2, 512], F32)) for b in range(4)]
        (score_0, score_1), (kqv_bank, probs_t_0), (probs_t_1, x1_bank), (x_bank, xn2_bank) = \
            [[w[:, b, :] for b in range(2)] for w in wide]
        score_bank, probs_t_bank = [score_0, score_1], [probs_t_0, probs_t_1]

        def up_banks(c, u):
            if isinstance(c, int) and c == 0:
                return wide[u % 2]
            return wide[(0, 1, 3)[u % 3]]

        down_bank = [probs_t_1, x1_bank]

        s_perm = sem("perm_loaded")
        s_wkq = sem("wkq_loaded")
        s_gates = sem("gates_loaded")
        s_wvs = sem("wv_wskip_loaded")
        s_up = sem("up_loaded")
        s_down = sem("down_loaded")
        s_zero = sem("dve_zeroed")
        s_ident = sem("identity_made")
        s_half = sem("constants_set")
        s_index = sem("index_made")
        s_tanh = sem("tanh_made")
        s_wkq_mm = sem("wkq_multiplied")
        s_wkq_sb = sem("wkq_ready")
        s_wvs_sb = sem("wv_wskip_ready")
        s_up_high = sem("up_high_ready")
        s_up_low = sem("up_low_ready")
        s_down_sb = sem("down_ready")
        s_head = [sem(f"x_head_gathered{t}") for t in range(NT)]
        s_rest = sem("x_rest_gathered")
        s_xstage = [sem(f"x_staged{s}") for s in range(2)]
        s_cstage = [sem(f"ctx_staged{s}") for s in range(2)]
        s_t0 = sem("x_transposed")
        s_xevac = sem("x_rows_stored")
        s_bn1a = sem("bn1_done")
        s_st1 = sem("stats1_done")
        s_var1 = sem("var1_done")
        s_rstd1 = sem("rstd1_done")
        s_xn = sem("xn_ready")
        s_kqv = sem("kq_v_multiplied")
        s_kq_sb = sem("kq_stored")
        s_vt_sb = sem("v_stored")
        s_score = sem("scores_ready")
        s_max = sem("max_ready")
        s_exp = sem("exp_done")
        s_inv = sem("inv_sum_ready")
        s_pn = sem("probs_normalised")
        s_pt = sem("probs_transposed")
        s_pt_sb = [sem(f"probs_t_stored{h}") for h in range(2)]
        s_skip = sem("skip_done")
        s_att = sem("attention_done")
        s_x1 = sem("x1_ready")
        s_bn2a = sem("bn2_done")
        s_st2 = sem("stats2_done")
        s_var2 = sem("var2_done")
        s_neg = sem("neg_mean2_ready")
        s_rstd2 = sem("rstd2_ready")
        s_xn2 = sem("xn2_ready")
        s_x1t = sem("x1_transposed")
        s_x1t_sb = sem("x1_t_stored")
        s_xn2t = sem("xn2_transposed")
        s_high = sem("high_ready")
        s_low = sem("low_ready")
        s_stack = [sem(f"stacked{s}") for s in range(2)]
        s_upmm = sem("up_multiplied")
        s_gelu = sem("gelu_done")
        s_downmm = sem("down_multiplied")
        s_res = sem("result_ready")
        s_out = sem("result_stored")

        block = es.enter_context(nc.Block())

        def pipeline(engine, step, end):
            for i in range(-2, 4):
                step(i, i % 4)
            with engine.Fori(1, PAIRS // 4 - 1) as k:
                for slot in range(4):
                    step(4 * k + slot, slot)
            for i in range(PAIRS - 4, end):
                step(i, i % 4)

        def in_place(i):
            return not isinstance(i, int) or i not in (0, 1)

        def has(q):
            return not isinstance(q, int) or 0 <= q < PAIRS

        def past(q, least):
            return not isinstance(q, int) or q >= least

        def pair_rows(q):
            return bass.ds(q * P, P)

        def staged(q, s, first=0):
            return 8 * (q - s - first) + 16

        def store_probs_t(engine, copy, q, s, h):
            if has(q):
                engine.wait_ge(s_pt, 2 * q + h + 1)
                if past(q, 2):
                    engine.wait_ge(s_att, q - 1)
                copy(probs_t[s][:, :, 2 * h:2 * h + 2, :].rearrange("m b t n -> m b (t n)"),
                     probs_t_bank[h].rearrange("m (b n) -> m b n", b=2)).then_inc(s_pt_sb[h], 1)

        def store_x1_t(engine, copy, q):
            if has(q):
                engine.wait_ge(s_x1t, q + 1)
                copy(xt[:, :, pair_rows(q)], x_bank.rearrange("p (t r) -> p t r", t=NT)).then_inc(s_x1t_sb, 1)

        def store_high(engine, copy, q, s):
            if has(q):
                engine.wait_ge(s_xn2t, q + 1)
                if past(q, 2):
                    engine.wait_ge(s_stack[s], PARTS * 8 * (q - s))
                copy(high[s][:, :, :], xn2_bank.rearrange("p (t r) -> p t r", t=NT)).then_inc(s_high, 1)

        @block.sync
        def _(sp):
            sp.dma_start(perm_sb[:, :], perm).then_inc(s_perm, 16)
            sp.dma_start(wq_sb[:, :], wq).then_inc(s_wkq, 16)
            sp.dma_start(gates_sb[:, :], gates.to_broadcast([P, 2])).then_inc(s_gates, 16)

            def stage_x(q, s):
                if has(q) and past(q, UNSTAGED):
                    if past(q, UNSTAGED + 2):
                        sp.wait_ge(s_t0, q - 1)
                    sp.wait_ge(s_rest, 16 * NT)
                    sp.dma_start(x_stage[:, s, :].rearrange("n (t r) -> n t r", t=NT), xt[:, :, pair_rows(q)])\
                      .then_inc(s_xstage[s], 16)

            def stage_ctx(q, s):
                if has(q):
                    if past(q, 2):
                        sp.wait_ge(s_kqv, q - 1)
                    sp.dma_start(ctx_stage[s][:, :], ctx[pair_rows(q), :]).then_inc(s_cstage[s], 16)

            def step(i, slot):
                s = slot % 2
                stage_ctx(i + 2, s)
                if isinstance(i, int) and i == -2:
                    for b in range(2):
                        half = slice(b * C, (b + 1) * C)
                        sp.dma_start(wv_raw[half, b, :], wv_t).then_inc(s_wvs, 16)
                        sp.dma_start(ws_raw[half, b, :], wskip_t).then_inc(s_wvs, 16)
                if isinstance(i, int) and i == -1:
                    for part in range(PARTS):
                        sp.dma_start(up_raw[part * DH:(part + 1) * DH, :, :], up)\
                          .then_inc(s_up, 16)
                if isinstance(i, int) and i == 1:
                    sp.dma_start(down_sb[:, :, :], down.rearrange("h m d -> m h d")).then_inc(s_down, 16)
                if has(i - 3):
                    q, o = i - 3, 1 - s
                    sp.wait_ge(s_low, q + 1)
                    if isinstance(q, int) and q == PAIRS - LATE:
                        sp.wait_ge(s_att, PAIRS)
                    for part, src in enumerate((high, low, high, low)):
                        group = slice(part * DH, (part + 1) * DH)
                        if isinstance(q, int) and q >= PAIRS - LATE:
                            to = late[group, :, q - (PAIRS - LATE), :]
                        else:
                            to = stack[group, :, bass.ds(q, 1), :].rearrange("p g a n -> p g (a n)")
                        sp.dma_start(to.bitcast(F32), src[o][:, :, :].rearrange("p t r -> p (t r)").bitcast(F32))\
                          .then_inc(s_stack[o], 16)
                stage_x(i + 4, s)

            pipeline(sp, step, PAIRS + 3)

        @block.gpsimd
        def _(pool):
            pool.memset(ident[:, :], 0.0).then_inc(s_ident, 1)
            pool.memset(minus_half[:, :], -0.5).then_inc(s_half, 1)
            pool.memset(minus_one[:, :], -1.0).then_inc(s_half, 1)
            pool.memset(eps[:, :], EPS).then_inc(s_half, 1)
            pool.wait_ge(s_ident, 1)
            pool.affine_select(out=ident[:, :], in_=ident[:, :], compare_op=ALU.not_equal, fill=1.0,
                               base=0, pattern=[[-1, P]], channel_multiplier=1).then_inc(s_ident, 1)
            pool.wait_ge(s_perm, 16)
            for t in range(NT):
                pool.indirect_dma_start(
                    xt[:, t, 0:HEAD_ROWS], None, x_head,
                    bass.IndirectOffsetOnAxis(ap=perm_sb[:, t:t + 1].bitcast(U32), axis=0)).then_inc(s_head[t], 16)

            def gather_rest(t):
                pool.indirect_dma_start(
                    xt[:, t, HEAD_ROWS:ROWS], None, x_rest,
                    bass.IndirectOffsetOnAxis(ap=perm_sb[:, t:t + 1].bitcast(U32), axis=0)).then_inc(s_rest, 16)

            pool.wait_ge(s_half, 3)

            def rstd(var, stats, to, done_var, done, q):
                pool.tensor_tensor(var[:, :], stats[:, 1:2], eps[:, :], ALU.add).then_inc(done_var, 1)
                pool.wait_ge(done_var, q + 1)
                pool.tensor_tensor(to[:, :], var[:, :], minus_half[:, :], ALU.pow).then_inc(done, 1)

            def normalise(q, h):
                if has(q):
                    pool.wait_ge(s_inv, 2 * q + h + 1)
                    if past(q, 1):
                        pool.wait_ge(s_pt, 2 * q + h - 1)
                    pool.tensor_tensor(pn[h][:, :, :], probs[h][:, :, :],
                                       inv_sum[h][:, :].unsqueeze(2).to_broadcast([P, 4, M]),
                                       ALU.mult).then_inc(s_pn, 1)

            def step(i, slot):
                s = slot % 2
                if has(i - 2):
                    q = i - 2
                    pool.wait_ge(s_st2, q + 1)
                    if past(q, 1):
                        pool.wait_ge(s_xn2t, q)
                    pool.tensor_tensor(neg_mean2[s][:, :], stats2[s][:, 0:1], minus_one[:, :], ALU.mult)\
                        .then_inc(s_neg, 1)
                    rstd(var2, stats2[s], rstd2[s], s_var2, s_rstd2, q)
                    pool.wait_ge(s_half, 3)
                    pool.wait_ge(s_rstd2, q + 1)
                    pool.wait_ge(s_neg, q + 1)
                    pool.tensor_scalar(xn2[:, :].rearrange("p (t d g) -> p t g d", t=NT, g=HPT),
                                       x1[s][:, :].rearrange("p (t g d) -> p t g d", t=NT, g=HPT),
                                       neg_mean2[s][:, 0:1], rstd2[s][:, 0:1], ALU.add, ALU.mult).then_inc(s_xn2, 1)
                if has(i + 1):
                    q, o = i + 1, 1 - s
                    pool.wait_ge(s_st1, q + 1)
                    rstd(var1, stats1[o], rstd1[o], s_var1, s_rstd1, q)
                if isinstance(i, int) and i == -1:
                    gather_rest(0)
                    gather_rest(1)
                if isinstance(i, int) and i == 0:
                    gather_rest(2)
                normalise(i, 0)
                normalise(i, 1)
                if isinstance(i, int) and i == 0:
                    gather_rest(3)

            pipeline(pool, step, PAIRS + 2)

            pool.wait_ge(s_index, CHUNKS)
            for c in range(CHUNKS):
                for t in range(NT):
                    tile = c * NT + t
                    pool.wait_ge(s_res, tile + 1)
                    pool.indirect_dma_start(
                        out, bass.IndirectOffsetOnAxis(ap=out_index[:, c, t:t + 1].bitcast(U32), axis=0),
                        xt[:, t, c * CH:(c + 1) * CH], None).then_inc(s_out, 16)
            pool.wait_ge(s_out, 16 * CHUNKS * NT)

        @block.tensor
        def _(pe):
            pe.wait_ge(s_ident, 2)
            pe.wait_ge(s_wkq, 48)
            pe.matmul(kqv_bank[:, 0:C], wk_sb[:, :, :].rearrange("o b c -> o (b c)"), wq_sb[:, :],
                      start=True, stop=True).then_inc(s_wkq_mm, 1)

            def warm(count):
                for _ in range(count):
                    pe.matmul(xn2_bank[:, 0:P], ident[:, :], ident[:, :], start=True, stop=True)

            warm(WARM_UP)

            def transposes(to, of):
                for t in range(NT):
                    last = pe.transpose(to[:, t * P:(t + 1) * P], of(t), ident[:, :])
                return last

            def scores(q, s, h):
                if has(q):
                    if h == 0:
                        if not past(q, 1):
                            pe.wait_ge(s_zero, 1)
                        pe.wait_ge(s_xn, q + 1)
                        pe.wait_ge(s_kq_sb, 2 * q + 2)
                    if past(q, 1):
                        pe.wait_ge(s_exp, 2 * q + h - 1)
                    for j in range(2):
                        t = 2 * h + j
                        last = pe.matmul(score_bank[h][:, j * 2 * M:(j + 1) * 2 * M], xn[s][:, t * P:(t + 1) * P],
                                         kq[s][:, :, :].rearrange("c b m -> c (b m)"), start=True, stop=True)
                    last.then_inc(s_score, 1)

            def probs_transposes(q, h):
                if has(q):
                    pe.wait_ge(s_pn, 2 * q + h + 1)
                    if past(q, 1):
                        pe.wait_ge(s_pt_sb[h], q)
                    for j in range(2):
                        for b in range(2):
                            at = (2 * b + j) * P
                            last = pe.transpose(probs_t_bank[h][:, at:at + P], pn[h][:, 2 * j + b, :], ident[:, :])
                    last.then_inc(s_pt, 1)

            def x_transposes(q, s):
                if has(q):
                    if past(q, 4):
                        pe.wait_ge(s_x1t_sb, q - 3)
                    elif past(q, 1):
                        pe.wait_ge(s_xevac, q)
                    if past(q, UNSTAGED):
                        pe.wait_ge(s_xstage[s], staged(q, s, UNSTAGED))
                        transposes(x_bank, lambda t: x_stage[:, s, t * P:(t + 1) * P]).then_inc(s_t0, 1)
                    else:
                        if q == PPC:
                            pe.wait_ge(s_rest, 16 * NT)
                        for t in range(NT):
                            if q == 0:
                                pe.wait_ge(s_head[t], 16)
                            last = pe.transpose(x_bank[:, t * P:(t + 1) * P], xt[:, t, q * P:(q + 1) * P], ident[:, :])
                        last.then_inc(s_t0, 1)

            def kq_and_v(q, s):
                if has(q):
                    pe.wait_ge(s_cstage[s], staged(q, s))
                    if past(q, 1):
                        pe.wait_ge(s_kq_sb, 2 * q)
                        pe.wait_ge(s_vt_sb, q)
                    else:
                        pe.wait_ge(s_wkq_sb, 2)
                        pe.wait_ge(s_wvs_sb, 2)
                    pe.matmul(kqv_bank[:, 0:M], wkq[:, :, :].rearrange("c b e -> c (b e)"), ctx_stage[s][:, :],
                              start=True, stop=True)
                    pe.matmul(kqv_bank[:, M:M + 2 * C], ctx_stage[s][:, :], wv_sb[:, :],
                              start=True, stop=True).then_inc(s_kqv, 1)

            def skip(q, s):
                if has(q):
                    if past(q, 1):
                        pe.wait_ge(s_x1, q)
                    pe.matmul(x1_bank, ws_sb[:, :], xn[s], start=True, stop=False,
                              skip_group_check=True).then_inc(s_skip, 1)

            def attention(q, s):
                if has(q):
                    pe.wait_ge(s_vt_sb, q + 1)
                    pe.wait_ge(s_pt_sb[0], q + 1)
                    pe.wait_ge(s_pt_sb[1], q + 1)
                    for b in range(2):
                        last = pe.matmul(x1_bank[b * C:(b + 1) * C, :], vt[s][:, b, :],
                                         probs_t[s][:, b, :, :].rearrange("m t n -> m (t n)"),
                                         start=False, stop=True, skip_group_check=True)
                    last.then_inc(s_att, 1)

            def x1_transposes(q, s):
                if has(q):
                    pe.wait_ge(s_x1, q + 1)
                    if has(q + 3):
                        pe.wait_ge(s_xevac, q + 4)
                    else:
                        pe.wait_ge(s_x1t_sb, q)
                    transposes(x_bank, lambda t: x1[s][:, t * P:(t + 1) * P]).then_inc(s_x1t, 1)

            def xn2_transposes(q):
                if has(q):
                    pe.wait_ge(s_xn2, q + 1)
                    if past(q, 1):
                        pe.wait_ge(s_low, q)
                    transposes(xn2_bank, lambda t: xn2[:, t * P:(t + 1) * P]).then_inc(s_xn2t, 1)

            def step(i, slot):
                s, o = slot % 2, (slot + 1) % 2
                scores(i, s, 0)
                probs_transposes(i - 1, 0)
                scores(i, s, 1)
                x1_transposes(i - 2, s)
                probs_transposes(i - 1, 1)
                if not isinstance(i, int) or i != 0:
                    kq_and_v(i + 1, o)
                skip(i - 1, o)
                attention(i - 1, o)
                if in_place(i):
                    x_transposes(i + 2, s)
                xn2_transposes(i - 2)
                if isinstance(i, int) and i == -1:
                    kq_and_v(1, 1)
                    x_transposes(2, 0)
                    warm(WARM_UP // 4)
                if isinstance(i, int) and i == 0:
                    x_transposes(3, 1)

            pipeline(pe, step, PAIRS)

            def up_unit(c, u):
                t, j = u // 2, u % 2
                if not isinstance(c, int) or c > 0 or u >= 2:
                    back = 2 if u < 2 or isinstance(c, int) and c == 0 else 3
                    pe.wait_ge(s_gelu, c * UNITS + u + 1 - back)
                for e in range(2):
                    g = 2 * j + e
                    w = up_w[:, g, t * MH:(t + 1) * MH]
                    rows = slice(t * P, (t + 1) * P)
                    if isinstance(c, int) and c == CHUNKS - 1:
                        last = pe.matmul(up_banks(c, u)[:, e, 0:LATE * P], w,
                                         stack[0:K_UP, g, PAIRS - 2 * LATE:PAIRS - LATE, rows], start=True, stop=True)
                        last = pe.matmul(up_banks(c, u)[:, e, LATE * P:CH], w, late[0:K_UP, g, :, rows],
                                         start=True, stop=True)
                    else:
                        last = pe.matmul(up_banks(c, u)[:, e, :], w, stack[0:K_UP, g, bass.ds(c * PPC, PPC), rows],
                                         start=True, stop=True)
                last.then_inc(s_upmm, 1)

            def down_tile(c, t):
                pe.wait_ge(s_gelu, c * UNITS + 2 * t + 2)
                if not isinstance(c, int) or c > 0 or t >= 2:
                    pe.wait_ge(s_res, c * NT + t - 1)
                for g in range(HPT):
                    last = pe.matmul(down_bank[t % 2][g * DH:(g + 1) * DH, :], down_sb[:, t * HPT + g, :],
                                     hidden[(2 * t + g // 2) % 4][:, g % 2, :],
                                     start=True, stop=True, skip_group_check=True)
                last.then_inc(s_downmm, 1)

            def stacked(c):
                for s in range(2):
                    pe.wait_ge(s_stack[s], (c + 1) * (PPC // 2 * PARTS * 16))

            def chunk(c):
                last = isinstance(c, int) and c + 1 == CHUNKS
                for t in range(NT):
                    if t + 1 < NT:
                        up_unit(c, 2 * t + 3)
                    if t + 2 < NT:
                        up_unit(c, 2 * t + 4)
                    if t + 1 == NT and not last:
                        up_unit(c + 1, 1)
                    down_tile(c, t)
                    if t + 2 == NT and not last:
                        stacked(c + 1)
                        up_unit(c + 1, 0)
                if not last:
                    up_unit(c + 1, 2)

            a, z = PAIRS - 2, PAIRS - 1
            probs_transposes(z, 0)
            pe.wait_ge(s_up_low, HPT)
            stacked(0)
            pe.wait_ge(s_exp, 2 * PAIRS)
            up_unit(0, 0)
            x1_transposes(a, a % 2)
            skip(z, z % 2)
            probs_transposes(z, 1)
            pe.wait_ge(s_vt_sb, PAIRS)
            pe.wait_ge(s_pt_sb[0], PAIRS)
            up_unit(0, 1)
            up_unit(0, 2)
            attention(z, z % 2)
            up_unit(0, 3)
            pe.wait_ge(s_down_sb, 1)
            down_tile(0, 0)
            up_unit(0, 4)
            xn2_transposes(a)
            x1_transposes(z, z % 2)
            up_unit(0, 5)
            down_tile(0, 1)
            up_unit(0, 6)
            up_unit(0, 7)
            xn2_transposes(z)
            down_tile(0, 2)
            stacked(1)
            up_unit(1, 0)
            up_unit(1, 1)
            down_tile(0, 3)
            pe.wait_ge(s_x1t_sb, PAIRS)
            pe.wait_ge(s_low, PAIRS)
            up_unit(1, 2)
            with pe.Fori(1, CHUNKS - 2) as c:
                chunk(c)
            chunk(CHUNKS - 2)
            chunk(CHUNKS - 1)

        @block.scalar
        def _(act):
            for b in range(2):
                act.dma_start(wk_sb[:, b, :], wk).then_inc(s_wkq, 16)
            act.wait_ge(s_gates, 16)
            act.activation(tanh_g[:, :], gates_sb[:, :], ACT.Tanh).then_inc(s_tanh, 1)
            act.wait_ge(s_wkq_mm, 1)
            act.activation(wkq[0:C, 0, :], kqv_bank[0:C, 0:C], ACT.Copy, scale=SCALE).then_inc(s_wkq_sb, 1)
            act.activation(wkq[C:P, 1, :], kqv_bank[C:P, 0:C], ACT.Copy, scale=SCALE).then_inc(s_wkq_sb, 1)

            def exps(q, h):
                if has(q):
                    act.wait_ge(s_max, 2 * q + h + 1)
                    if past(q, 1):
                        act.wait_ge(s_pn, 2 * q + h - 1)
                    for g in range(4):
                        last = act.activation(probs[h][:, g, :], score_bank[h][:, g * M:(g + 1) * M], ACT.Exp,
                                              bias=neg_max[h][:, g:g + 1], accum_out=sums[h][:, g:g + 1])
                    last.then_inc(s_exp, 1)

            def store_kq(q, s):
                if has(q):
                    act.wait_ge(s_kqv, q + 1)
                    if past(q, 2):
                        act.wait_ge(s_score, 2 * q - 2)
                    for b in range(2):
                        half = slice(b * C, (b + 1) * C)
                        act.activation(kq[s][half, b, :], kqv_bank[half, 0:M], ACT.Copy).then_inc(s_kq_sb, 1)

            def store_v(q, s):
                if has(q):
                    if past(q, 2):
                        act.wait_ge(s_att, q - 1)
                    act.activation(vt[s][:, :, :].rearrange("m b c -> m (b c)"), kqv_bank[:, M:M + 2 * C], ACT.Copy)\
                       .then_inc(s_vt_sb, 1)

            def store_x(q, slot):
                if has(q):
                    act.wait_ge(s_t0, q + 1)
                    if past(q, 4):
                        act.wait_ge(s_x1, q - 3)
                    act.activation(x_rows[:, slot, :], x_bank, ACT.Copy).then_inc(s_xevac, 1)

            def copy(to, of):
                return act.activation(to, of, ACT.Copy)

            def step(i, slot):
                s, o = slot % 2, (slot + 1) % 2
                exps(i, 0)
                store_probs_t(act, copy, i - 1, o, 1)
                if not isinstance(i, int) or i != 0:
                    store_kq(i + 1, o)
                store_x1_t(act, copy, i - 2)
                exps(i, 1)
                if not isinstance(i, int) or i != 0:
                    store_v(i + 1, o)
                if in_place(i):
                    store_x(i + 2, (slot + 2) % 4)
                if isinstance(i, int) and i == -1:
                    store_kq(1, 1)
                    store_v(1, 1)
                    store_x(2, 2)
                    act.wait_ge(s_up, 16 * PARTS)
                    act.activation(up_w[:, :, :], up_raw[:, :, :], ACT.Copy).then_inc(s_up_high, 1)
                if isinstance(i, int) and i == 0:
                    store_x(3, 3)
                store_high(act, copy, i - 2, s)

            pipeline(act, step, PAIRS)

            def gelus(c):
                for u in range(UNITS):
                    act.wait_ge(s_upmm, c * UNITS + u + 1)
                    if not isinstance(c, int) or u >= 4:
                        act.wait_ge(s_downmm, c * NT + u // 2 - 1)
                    elif u == 1:
                        act.wait_ge(s_x1, PAIRS - 2)
                    elif u == 2:
                        act.wait_ge(s_skip, PAIRS)
                    elif u == 3:
                        act.wait_ge(s_x1, PAIRS)
                    act.activation(hidden[u % 4], up_banks(c, u)[:, :, :], ACT.Gelu).then_inc(s_gelu, 1)

            gelus(0)
            with act.Fori(1, CHUNKS) as c:
                gelus(c)

        @block.vector
        def _(dve):
            dve.memset(kq[0][0:C, 1, :], 0.0)
            dve.memset(kq[0][C:P, 0, :], 0.0)
            dve.memset(kq[1][0:C, 1, :], 0.0)
            dve.memset(kq[1][C:P, 0, :], 0.0)
            for w in (wkq, wv_raw, ws_raw):
                dve.memset(w[0:C, 1, :], 0.0)
                last = dve.memset(w[C:P, 0, :], 0.0)
            last.then_inc(s_zero, 1)
            dve.wait_ge(s_zero, 1)
            dve.wait_ge(s_tanh, 1)
            dve.wait_ge(s_wvs, 64)
            for to, w in ((wv_sb, wv_raw), (ws_sb, ws_raw)):
                dve.tensor_scalar(to[:, :], w[:, :, :].rearrange("p b c -> p (b c)"), tanh_g[:, 0:1], None, ALU.mult)\
                   .then_inc(s_wvs_sb, 1)

            dve.wait_ge(s_perm, 16)
            for c in range(CHUNKS):
                dve.tensor_scalar(out_index[:, c, :], perm_sb[:, :], float(c * N), None, ALU.add)\
                   .then_inc(s_index, 1)

            def maxima(q, h):
                if has(q):
                    dve.wait_ge(s_score, 2 * q + h + 1)
                    dve.tensor_reduce(neg_max[h][:, :], score_bank[h].rearrange("n (g m) -> n g m", g=4),
                                      AX.X, ALU.max, negate=True).then_inc(s_max, 1)

            def inverses(q, h):
                if has(q):
                    dve.wait_ge(s_exp, 2 * q + h + 1)
                    dve.reciprocal(inv_sum[h][:, :], sums[h][:, :]).then_inc(s_inv, 1)

            def aggregate(bn, stats, done_bn, done, q):
                if has(q):
                    dve.wait_ge(s_zero, 1)
                    dve.wait_ge(done_bn, q + 1)
                    dve.bn_aggr(stats[:, :], bn[:, :]).then_inc(done, 1)

            def x_stats(q, slot):
                if has(q):
                    dve.wait_ge(s_xevac, q + 1)
                    if past(q, 1):
                        dve.wait_ge(s_st1, q)
                    if past(q, 2):
                        dve.wait_ge(s_xn, q - 1)
                    dve.bn_stats(bn1[:, :], x_rows[:, slot, :]).then_inc(s_bn1a, 1)

            def layernorm(q, slot):
                if has(q):
                    s = slot % 2
                    dve.wait_ge(s_rstd1, q + 1)
                    if past(q, 2):
                        dve.wait_ge(s_skip, q - 1)
                    dve.tensor_scalar(xn[s], x_rows[:, slot, :], stats1[s][:, 0:1], rstd1[s][:, 0:1],
                                      ALU.subtract, ALU.mult).then_inc(s_xn, 1)

            def residual(q, slot):
                if has(q):
                    dve.wait_ge(s_att, q + 1)
                    if past(q, 2):
                        dve.wait_ge(s_x1t, q - 1)
                        dve.wait_ge(s_xn2, q - 1)
                    dve.tensor_tensor(x1[slot % 2][:, :], x_rows[:, slot, :], x1_bank, ALU.add).then_inc(s_x1, 1)

            def x1_stats(q, s):
                if has(q):
                    dve.wait_ge(s_x1, q + 1)
                    if past(q, 1):
                        dve.wait_ge(s_st2, q)
                    dve.bn_stats(bn2[:, :], x1[s][:, :]).then_inc(s_bn2a, 1)

            def store_low(q, s):
                if has(q):
                    dve.wait_ge(s_high, q + 1)
                    dve.tensor_tensor(low[s][:, :, :], xn2_bank.rearrange("p (t r) -> p t r", t=NT),
                                      high[s][:, :, :].bitcast(F32), ALU.subtract).then_inc(s_low, 1)

            def up_low(g):
                last_copies = slice(2 * DH, K_UP)
                dve.wait_ge(s_up_high, 1)
                dve.tensor_tensor(up_w[last_copies, g, :], up_raw[last_copies, g, :],
                                  up_w[last_copies, g, :].bitcast(F32), ALU.subtract).then_inc(s_up_low, 1)

            def step(i, slot):
                s, o = slot % 2, (slot + 1) % 2
                if isinstance(i, int) and i == 0:
                    x_stats(1, 1)
                    aggregate(bn1, stats1[1], s_bn1a, s_st1, 1)
                    maxima(0, 0)
                    layernorm(1, 1)
                    maxima(0, 1)
                    inverses(0, 0)
                    up_low(0)
                    up_low(1)
                    inverses(0, 1)
                    up_low(2)
                    return
                x1_stats(i - 2, s)
                maxima(i, 0)
                aggregate(bn2, stats2[s], s_bn2a, s_st2, i - 2)
                x_stats(i + 1, (slot + 1) % 4)
                aggregate(bn1, stats1[o], s_bn1a, s_st1, i + 1)
                store_low(i - 3, o)
                store_probs_t(dve, dve.tensor_copy, i - 1, o, 0)
                maxima(i, 1)
                inverses(i, 0)
                layernorm(i + 1, (slot + 1) % 4)
                residual(i - 1, (slot - 1) % 4)
                inverses(i, 1)
                if isinstance(i, int) and i == 3:
                    up_low(3)
                if isinstance(i, int) and i == PAIRS - 4:
                    dve.wait_ge(s_down, 16)
                    dve.tensor_scalar(down_sb[:, :, :], down_sb[:, :, :], tanh_g[:, 1:2], None, ALU.mult)\
                       .then_inc(s_down_sb, 1)

            pipeline(dve, step, PAIRS)

            def result(c, t):
                dve.wait_ge(s_downmm, c * NT + t + 1)
                tile = xt[:, t:t + 1, bass.ds(c * CH, CH)]
                dve.tensor_tensor(tile, down_bank[t % 2].rearrange("p (a r) -> p a r", a=1), tile, ALU.add)\
                   .then_inc(s_res, 1)

            a, z = PAIRS - 2, PAIRS - 1
            store_probs_t(dve, dve.tensor_copy, z, z % 2, 0)
            x1_stats(a, a % 2)
            store_x1_t(dve, dve.tensor_copy, a)
            aggregate(bn2, stats2[a % 2], s_bn2a, s_st2, a)
            store_probs_t(dve, dve.tensor_copy, z, z % 2, 1)
            store_low(a - 1, z % 2)
            residual(z, z % 4)
            x1_stats(z, z % 2)
            dve.wait_ge(s_x1t_sb, PPC)
            result(0, 0)
            aggregate(bn2, stats2[z % 2], s_bn2a, s_st2, z)
            store_high(dve, dve.tensor_copy, a, a % 2)
            store_x1_t(dve, dve.tensor_copy, z)
            store_low(a, a % 2)
            result(0, 1)
            store_high(dve, dve.tensor_copy, z, z % 2)
            store_low(z, z % 2)
            result(0, 2)
            result(0, 3)
            dve.wait_ge(s_x1t_sb, PAIRS)
            with dve.Fori(1, CHUNKS) as c:
                for t in range(NT):
                    result(c, t)


def kernel(x, ctx_1024, g_xattn, g_ffn, L0_xattn_Wq, L0_xattn_Wk, L0_xattn_Wv, L0_xattn_Wskip,
           L0_ffn_up, L0_ffn_down, L0_ffn_perm):
    import numpy as np
    from concourse import bacc
    from concourse.bass_utils import run_bass_kernel_spmd

    batches, channels, n = x.shape
    rows = batches * channels
    head = 512
    dh, mh = L0_ffn_up.shape[1:]
    xt = np.asarray(x).reshape(rows, n).T
    ins = {
        "x_head": xt[:, :head],
        "x_rest": xt[:, head:],
        "ctx": np.asarray(ctx_1024).reshape(rows, -1),
        "perm": np.asarray(L0_ffn_perm).astype(np.int32).reshape(n // 128, 128).T,
        "gates": np.concatenate([np.asarray(g_xattn), np.asarray(g_ffn)]).reshape(1, 2),
        "wq": L0_xattn_Wq,
        "wk": L0_xattn_Wk,
        "wv_t": np.asarray(L0_xattn_Wv).T,
        "wskip_t": np.asarray(L0_xattn_Wskip).T,
        "up": np.asarray(L0_ffn_up).reshape(n // 128, 128 // dh, dh, mh)\
            .transpose(2, 1, 0, 3).reshape(dh, 128 // dh, -1),
        "down": L0_ffn_down,
    }
    nc = bacc.Bacc("TRN2", target_bir_lowering=False, num_devices=1)
    arrays, args = {}, {}
    for name, a in ins.items():
        a = np.ascontiguousarray(a)
        arrays[f"in_{name}"] = a
        args[name] = nc.dram_tensor(f"in_{name}", a.shape, mybir.dt.from_np(a.dtype), kind="ExternalInput").ap()
    chunk = 512
    out = nc.dram_tensor("out_0", (rows // chunk * n, chunk), F32, kind="ExternalOutput").ap()
    build_block(nc, out=out, **args)
    r = run_bass_kernel_spmd(nc, [arrays], core_ids=[0])
    y = r.results[0]["out_0"].reshape(rows // chunk, n, chunk)
    return np.ascontiguousarray(y.transpose(0, 2, 1)).reshape(batches, channels, n)
```
